# Optimizing a Trainium2 kernel written in Bass

```python
import numpy as np
import jax
import jax.numpy as jnp

def _softmax(x, axis=-1):
    return jax.nn.softmax(x, axis=axis)

def _gelu(x):
    return jax.nn.gelu(x, approximate=True)

def _silu(x):
    return jax.nn.silu(x)

def _sigmoid(x):
    return jax.nn.sigmoid(x)

def _layernorm(x, axis=-1, eps=1e-05):
    m = jnp.mean(x, axis=axis, keepdims=True)
    v = jnp.var(x, axis=axis, keepdims=True)
    return (x - m) / jnp.sqrt(v + eps)

def _scatter_add(tgt, idx, src, axis=0):
    return tgt.at[idx].add(src)

def _segment_sum(src, seg, n):
    return jax.ops.segment_sum(src, seg, n)
kernel_name = 'mk_gnn_resnorm_d4_gnn_r32_648007'

def setup_inputs(seed: int=0):
    np.random.seed(seed)
    _w = jnp.asarray

    def _rec_inputs():
        import jax
        import jax.numpy as jnp
        _gk = jax.random.key(seed)
        x = -0.0003713 + 1 * jax.random.normal(jax.random.fold_in(_gk, 1), (3125, 128), jnp.float32)
        _s = jax.random.randint(jax.random.fold_in(_gk, 2), (50000,), 0, 3125, jnp.int32)
        _d = jax.random.randint(jax.random.fold_in(_gk, 3), (50000,), 0, 3125, jnp.int32)
        _loop = jnp.arange(3125, dtype=jnp.int32)
        src = jnp.concatenate([_s, _d, _loop])
        dst = jnp.concatenate([_d, _s, _loop])
        _o = jnp.argsort(dst, stable=True)
        src = src[_o]
        dst = dst[_o]
        edge_type_1000 = jax.random.randint(jax.random.fold_in(_gk, 13), (103125,), 0, 1000, jnp.int32)
        edge_type_32 = jax.random.randint(jax.random.fold_in(_gk, 14), (103125,), 0, 32, jnp.int32)
        edge_type_8 = jax.random.randint(jax.random.fold_in(_gk, 15), (103125,), 0, 8, jnp.int32)
        edge_weight = jax.random.uniform(jax.random.fold_in(_gk, 16), (103125,), jnp.float32, 0.0, 0.999998)
        node_type_16 = jax.random.randint(jax.random.fold_in(_gk, 17), (3125,), 0, 16, jnp.int32)
        return (x, src, dst, edge_type_1000, edge_type_32, edge_type_8, edge_weight, node_type_16)
    x, src, dst, edge_type_1000, edge_type_32, edge_type_8, edge_weight, node_type_16 = _rec_inputs()

    def _L0_gnn_setup():
        import jax, jax.numpy as jnp
        import numpy as np
        N_NODES = 3125
        N_REL = 1000
        N_EDGES = 50000
        EMB = 128
        key = jax.random.key(seed)
        k1, k2, k3, k4, k5 = jax.random.split(key, 5)
        inlayer = jax.random.normal(k1, (N_NODES, EMB), dtype=jnp.float32)
        dual_layer = jax.random.normal(k2, (N_REL, 2 * EMB), dtype=jnp.float32)
        edge_index = jax.random.randint(k3, (2, N_EDGES), 0, N_NODES, dtype=jnp.int64)
        rel_ids = jax.random.randint(k4, (N_EDGES,), 0, N_REL, dtype=jnp.int64)
        conv_w = jax.random.normal(k5, (2 * EMB, 1), dtype=jnp.float32) * 0.05
        conv_b = jnp.zeros((1,), dtype=jnp.float32)
        return {'inlayer': inlayer, 'dual_layer': dual_layer, 'edge_index': edge_index, 'rel_ids': rel_ids, 'conv_w': conv_w, 'conv_b': conv_b}
    _L0_gnn_all = _L0_gnn_setup()
    _L0_gnn_in = {k: v for k, v in _L0_gnn_all.items() if k in ('dual_layer', 'conv_w', 'conv_b')}
    del _L0_gnn_all

    def _L1_gnn_setup():
        import jax, jax.numpy as jnp
        import numpy as np
        N_NODES = 3125

        def gcn_conv(x, edge_index, W, b, n):
            h = x @ W
            src, dst = (edge_index[0], edge_index[1])
            loop = jnp.arange(n, dtype=edge_index.dtype)
            row = jnp.concatenate([src, loop])
            col = jnp.concatenate([dst, loop])
            ones = jnp.ones(row.shape[0], dtype=h.dtype)
            deg = jax.ops.segment_sum(ones, col, num_segments=n)
            dinv = jnp.where(deg > 0, jax.lax.rsqrt(deg), jnp.zeros_like(deg))
            norm = dinv[row] * dinv[col]
            msg = norm[:, None] * h[row]
            out = jax.ops.segment_sum(msg, col, num_segments=n)
            return out + b
        key = jax.random.key(seed)
        k1, k2, k3, k4 = jax.random.split(key, 4)
        d_in, d_hid, d_out = (128, 256, 128)
        x = jax.random.normal(k1, (N_NODES, d_in), dtype=jnp.float32)
        edge_index = jax.random.randint(k2, (2, 31250), 0, N_NODES, dtype=jnp.int32)
        lim1 = float(np.sqrt(6.0 / (d_in + d_hid)))
        lim2 = float(np.sqrt(6.0 / (d_hid + d_out)))
        W1 = jax.random.uniform(k3, (d_in, d_hid), jnp.float32, -lim1, lim1)
        b1 = jnp.zeros((d_hid,), jnp.float32)
        W2 = jax.random.uniform(k4, (d_hid, d_out), jnp.float32, -lim2, lim2)
        b2 = jnp.zeros((d_out,), jnp.float32)
        return {'x': x, 'edge_index': edge_index, 'W1': W1, 'b1': b1, 'W2': W2, 'b2': b2}
    _L1_gnn_all = _L1_gnn_setup()
    _L1_gnn_in = {k: v for k, v in _L1_gnn_all.items() if k in ('W1', 'b1', 'W2', 'b2')}
    del _L1_gnn_all

    def _L2_gnn_setup():
        import jax, jax.numpy as jnp
        import numpy as np
        N_NODES = 50000
        N_EDGES = 25000
        IN_DIM = 128
        OUT_DIM = 128
        NUM_RELS = 8
        key = jax.random.key(seed)
        k_feat, k_rel, k_w, k_src, k_dst, k_rt = jax.random.split(key, 6)
        feat = jax.random.normal(k_feat, (N_NODES, IN_DIM), dtype=jnp.float32)
        limit = float(np.sqrt(6.0 / (IN_DIM + OUT_DIM)))
        rel_emb = jax.random.uniform(k_rel, (NUM_RELS, IN_DIM, OUT_DIM), dtype=jnp.float32, minval=-limit, maxval=limit)
        edge_weight = jax.random.uniform(k_w, (N_EDGES,), dtype=jnp.float32)
        src = jax.random.randint(k_src, (N_EDGES,), 0, N_NODES, dtype=jnp.int32)
        dst = jax.random.randint(k_dst, (N_EDGES,), 0, N_NODES, dtype=jnp.int32)
        rel_type = jax.random.randint(k_rt, (N_EDGES,), 0, NUM_RELS, dtype=jnp.int32)
        return {'feat': feat, 'rel_emb': rel_emb, 'edge_weight': edge_weight, 'src': src, 'dst': dst, 'rel_type': rel_type}
    _L2_gnn_all = _L2_gnn_setup()
    _L2_gnn_in = {k: v for k, v in _L2_gnn_all.items() if k in ('rel_emb',)}
    del _L2_gnn_all

    def _L3_gnn_setup():
        import jax, jax.numpy as jnp
        import numpy as np
        N = 625
        E = 10000
        DIN = 128
        HID = 128
        H = 8
        HS = HID // H
        NT = 16
        RT = 32
        L = 2
        OUT = 128
        SQRT_D = float(np.sqrt(HS))

        def typed_linear(x, t, W):
            y_all = jnp.einsum('nd,tdo->nto', x, W)
            return jnp.take_along_axis(y_all, t[:, None, None], axis=1)[:, 0]

        def edge_softmax(a, dst, n):
            amax = jax.ops.segment_max(a, dst, num_segments=n)
            ex = jnp.exp(a - amax[dst])
            s = jax.ops.segment_sum(ex, dst, num_segments=n)
            return ex / s[dst]

        def gt_layer(x, ntype, etype, src, dst, Wk, Wq, Wv, Wa, Watt, Wmsg, pri, skip, g, b):
            n = x.shape[0]
            k = typed_linear(x, ntype, Wk).reshape(n, H, HS)
            q = typed_linear(x, ntype, Wq).reshape(n, H, HS)
            v = typed_linear(x, ntype, Wv).reshape(n, H, HS)
            kT = jnp.einsum('nhd,htdo->nhto', k, Watt)
            vT = jnp.einsum('nhd,htdo->nhto', v, Wmsg)
            kw = kT[src, :, etype]
            m = vT[src, :, etype]
            a = jnp.einsum('ehd,ehd->eh', kw, q[dst]) * pri[:, etype].T / SQRT_D
            att = edge_softmax(a, dst, n)
            msg = (m * att[:, :, None]).reshape(-1, H * HS)
            hag = jax.ops.segment_sum(msg, dst, num_segments=n)
            h = jax.nn.silu(typed_linear(hag, ntype, Wa))
            alpha = jax.nn.sigmoid(skip[ntype])[:, None]
            h = h * alpha + x * (1.0 - alpha)
            mu = jnp.mean(h, axis=-1, keepdims=True)
            var = jnp.mean((h - mu) ** 2, axis=-1, keepdims=True)
            return (h - mu) * jax.lax.rsqrt(var + 1e-05) * g + b
        key = jax.random.key(seed)
        ks = jax.random.split(key, 16)
        f32 = jnp.float32
        return {'x': jax.random.normal(ks[0], (N, DIN), f32), 'ntype': jax.random.randint(ks[1], (N,), 0, NT), 'etype': jax.random.randint(ks[2], (E,), 0, RT), 'src': jax.random.randint(ks[3], (E,), 0, N), 'dst': jax.random.randint(ks[4], (E,), 0, N), 'Wk': jax.random.normal(ks[5], (L, NT, DIN, HID), f32) / np.sqrt(DIN), 'Wq': jax.random.normal(ks[6], (L, NT, DIN, HID), f32) / np.sqrt(DIN), 'Wv': jax.random.normal(ks[7], (L, NT, DIN, HID), f32) / np.sqrt(DIN), 'Wa': jax.random.normal(ks[8], (L, NT, HID, HID), f32) / np.sqrt(HID), 'Watt': jax.random.normal(ks[9], (L, H, RT, HS, HS), f32) / np.sqrt(HS), 'Wmsg': jax.random.normal(ks[10], (L, H, RT, HS, HS), f32) / np.sqrt(HS), 'pri': jnp.ones((L, H, RT), f32), 'skip': jnp.ones((L, NT), f32), 'ln_g': jnp.ones((L, HID), f32), 'ln_b': jnp.zeros((L, HID), f32), 'ff_w': jax.random.normal(ks[11], (HID, OUT), f32) / np.sqrt(HID), 'ff_b': jnp.zeros((OUT,), f32)}
    _L3_gnn_all = _L3_gnn_setup()
    _L3_gnn_in = {k: v for k, v in _L3_gnn_all.items() if k in ('Wk', 'Wq', 'Wv', 'Wa', 'Watt', 'Wmsg', 'pri', 'skip', 'ln_g', 'ln_b', 'ff_w', 'ff_b')}
    del _L3_gnn_all
    return {'x': x, 'src': src, 'dst': dst, 'edge_type_1000': edge_type_1000, 'edge_type_32': edge_type_32, 'edge_type_8': edge_type_8, 'edge_weight': edge_weight, 'node_type_16': node_type_16, 'L0_gnn_dual_layer': _L0_gnn_in['dual_layer'], 'L0_gnn_conv_w': _L0_gnn_in['conv_w'], 'L0_gnn_conv_b': _L0_gnn_in['conv_b'], 'L1_gnn_W1': _L1_gnn_in['W1'], 'L1_gnn_b1': _L1_gnn_in['b1'], 'L1_gnn_W2': _L1_gnn_in['W2'], 'L1_gnn_b2': _L1_gnn_in['b2'], 'L2_gnn_rel_emb': _L2_gnn_in['rel_emb'], 'L3_gnn_Wk': _L3_gnn_in['Wk'], 'L3_gnn_Wq': _L3_gnn_in['Wq'], 'L3_gnn_Wv': _L3_gnn_in['Wv'], 'L3_gnn_Wa': _L3_gnn_in['Wa'], 'L3_gnn_Watt': _L3_gnn_in['Watt'], 'L3_gnn_Wmsg': _L3_gnn_in['Wmsg'], 'L3_gnn_pri': _L3_gnn_in['pri'], 'L3_gnn_skip': _L3_gnn_in['skip'], 'L3_gnn_ln_g': _L3_gnn_in['ln_g'], 'L3_gnn_ln_b': _L3_gnn_in['ln_b'], 'L3_gnn_ff_w': _L3_gnn_in['ff_w'], 'L3_gnn_ff_b': _L3_gnn_in['ff_b']}

def reference(x, src, dst, edge_type_1000, edge_type_32, edge_type_8, edge_weight, node_type_16, L0_gnn_dual_layer, L0_gnn_conv_w, L0_gnn_conv_b, L1_gnn_W1, L1_gnn_b1, L1_gnn_W2, L1_gnn_b2, L2_gnn_rel_emb, L3_gnn_Wk, L3_gnn_Wq, L3_gnn_Wv, L3_gnn_Wa, L3_gnn_Watt, L3_gnn_Wmsg, L3_gnn_pri, L3_gnn_skip, L3_gnn_ln_g, L3_gnn_ln_b, L3_gnn_ff_w, L3_gnn_ff_b):
    import jax
    import jax.numpy as jnp

    def _L0_gnn_ref(inlayer, dual_layer, edge_index, rel_ids, conv_w, conv_b):
        import jax, jax.numpy as jnp
        import numpy as np
        N_NODES = 3125
        N_REL = 1000
        N_EDGES = 50000
        EMB = 128
        N = inlayer.shape[0]
        dual_transform = (dual_layer @ conv_w + conv_b).reshape(-1)
        logits = dual_transform[rel_ids]
        lrelu = jax.nn.leaky_relu(logits, negative_slope=0.01)
        rows = edge_index[0]
        cols = edge_index[1]
        row_max = jax.ops.segment_max(lrelu, rows, num_segments=N)
        ex = jnp.exp(lrelu - row_max[rows])
        row_sum = jax.ops.segment_sum(ex, rows, num_segments=N)
        coefs = ex / row_sum[rows]
        msgs = coefs[:, None] * inlayer[cols]
        out = jax.ops.segment_sum(msgs, rows, num_segments=N)
        return jax.nn.relu(out)

    def _L1_gnn_ref(x, edge_index, W1, b1, W2, b2):
        import jax, jax.numpy as jnp
        import numpy as np
        N_NODES = 3125

        def gcn_conv(x, edge_index, W, b, n):
            h = x @ W
            src, dst = (edge_index[0], edge_index[1])
            loop = jnp.arange(n, dtype=edge_index.dtype)
            row = jnp.concatenate([src, loop])
            col = jnp.concatenate([dst, loop])
            ones = jnp.ones(row.shape[0], dtype=h.dtype)
            deg = jax.ops.segment_sum(ones, col, num_segments=n)
            dinv = jnp.where(deg > 0, jax.lax.rsqrt(deg), jnp.zeros_like(deg))
            norm = dinv[row] * dinv[col]
            msg = norm[:, None] * h[row]
            out = jax.ops.segment_sum(msg, col, num_segments=n)
            return out + b
        n = x.shape[0]
        h = jax.nn.relu(gcn_conv(x, edge_index, W1, b1, n))
        h = jax.nn.relu(gcn_conv(h, edge_index, W2, b2, n))
        return h

    def _L2_gnn_ref(feat, rel_emb, edge_weight, src, dst, rel_type):
        import jax, jax.numpy as jnp
        import numpy as np
        N_NODES = 50000
        N_EDGES = 25000
        IN_DIM = 128
        OUT_DIM = 128
        NUM_RELS = 8
        src_feat = feat[src]
        num_rels = rel_emb.shape[0]
        msg = jnp.zeros((src_feat.shape[0], rel_emb.shape[2]), dtype=src_feat.dtype)
        for r in range(num_rels):
            mask = (rel_type == r)[:, None]
            msg = msg + jnp.where(mask, src_feat @ rel_emb[r], jnp.zeros((), dtype=src_feat.dtype))
        msg = msg * edge_weight[:, None]
        return jax.ops.segment_sum(msg, dst, num_segments=feat.shape[0])

    def _L3_gnn_ref(x, ntype, etype, src, dst, Wk, Wq, Wv, Wa, Watt, Wmsg, pri, skip, ln_g, ln_b, ff_w, ff_b):
        import jax, jax.numpy as jnp
        import numpy as np
        N = 625
        E = 10000
        DIN = 128
        HID = 128
        H = 8
        HS = HID // H
        NT = 16
        RT = 32
        L = 2
        OUT = 128
        SQRT_D = float(np.sqrt(HS))

        def typed_linear(x, t, W):
            y_all = jnp.einsum('nd,tdo->nto', x, W)
            return jnp.take_along_axis(y_all, t[:, None, None], axis=1)[:, 0]

        def edge_softmax(a, dst, n):
            amax = jax.ops.segment_max(a, dst, num_segments=n)
            ex = jnp.exp(a - amax[dst])
            s = jax.ops.segment_sum(ex, dst, num_segments=n)
            return ex / s[dst]

        def gt_layer(x, ntype, etype, src, dst, Wk, Wq, Wv, Wa, Watt, Wmsg, pri, skip, g, b):
            n = x.shape[0]
            k = typed_linear(x, ntype, Wk).reshape(n, H, HS)
            q = typed_linear(x, ntype, Wq).reshape(n, H, HS)
            v = typed_linear(x, ntype, Wv).reshape(n, H, HS)
            kT = jnp.einsum('nhd,htdo->nhto', k, Watt)
            vT = jnp.einsum('nhd,htdo->nhto', v, Wmsg)
            kw = kT[src, :, etype]
            m = vT[src, :, etype]
            a = jnp.einsum('ehd,ehd->eh', kw, q[dst]) * pri[:, etype].T / SQRT_D
            att = edge_softmax(a, dst, n)
            msg = (m * att[:, :, None]).reshape(-1, H * HS)
            hag = jax.ops.segment_sum(msg, dst, num_segments=n)
            h = jax.nn.silu(typed_linear(hag, ntype, Wa))
            alpha = jax.nn.sigmoid(skip[ntype])[:, None]
            h = h * alpha + x * (1.0 - alpha)
            mu = jnp.mean(h, axis=-1, keepdims=True)
            var = jnp.mean((h - mu) ** 2, axis=-1, keepdims=True)
            return (h - mu) * jax.lax.rsqrt(var + 1e-05) * g + b
        h = x
        for l in range(L):
            h = gt_layer(h, ntype, etype, src, dst, Wk[l], Wq[l], Wv[l], Wa[l], Watt[l], Wmsg[l], pri[l], skip[l], ln_g[l], ln_b[l])
        return h @ ff_w + ff_b
    edge_index = jnp.stack([src, dst])
    x = _layernorm(x + _L0_gnn_ref(x, L0_gnn_dual_layer, edge_index, edge_type_1000, L0_gnn_conv_w, L0_gnn_conv_b), axis=-1)
    x = _layernorm(x + _L1_gnn_ref(x, edge_index, L1_gnn_W1, L1_gnn_b1, L1_gnn_W2, L1_gnn_b2), axis=-1)
    x = _layernorm(x + _L2_gnn_ref(x, L2_gnn_rel_emb, edge_weight, src, dst, edge_type_8), axis=-1)
    x = _layernorm(x + _L3_gnn_ref(x, node_type_16, edge_type_32, src, dst, L3_gnn_Wk, L3_gnn_Wq, L3_gnn_Wv, L3_gnn_Wa, L3_gnn_Watt, L3_gnn_Wmsg, L3_gnn_pri, L3_gnn_skip, L3_gnn_ln_g, L3_gnn_ln_b, L3_gnn_ff_w, L3_gnn_ff_b), axis=-1)
    return x

_drawn_inputs = setup_inputs


def setup_inputs(seed=0):
    import zlib

    import numpy as np

    out = dict(_drawn_inputs(seed))
    spreads = {'L1_gnn_b1': (0.0, 0.1),
     'L1_gnn_b2': (0.0, 0.1),
     'L3_gnn_pri': (1.0, 0.2),
     'L3_gnn_skip': (1.0, 0.2),
     'L3_gnn_ln_g': (1.0, 0.2),
     'L3_gnn_ln_b': (0.0, 0.1),
     'L3_gnn_ff_b': (0.0, 0.1)}
    factors = {}
    for name, (base, spread) in spreads.items():
        noise = np.random.default_rng([zlib.crc32(name.encode()), seed]).standard_normal(out[name].shape)
        drawn = base * np.exp(spread * noise) if base else spread * noise
        out[name] = jnp.asarray(drawn.astype(out[name].dtype))
    for name, factor in factors.items():
        out[name] = (out[name] * factor).astype(out[name].dtype)
    return out
```

```python
from contextlib import ExitStack

import numpy as np

import concourse.bass as bass
from concourse import mybir

F32, BF16, I32, U32 = mybir.dt.float32, mybir.dt.bfloat16, mybir.dt.int32, mybir.dt.uint32
ALU = mybir.AluOpType
ACT = mybir.ActivationFunctionType
AX_X = mybir.AxisListType.X

P = 128
N_NODES, D, N_EDGES = 3125, 128, 103125
NT = -(-N_NODES // P)
N_PAD = NT * P
N_REL, HID = 1000, 256
R8, R16, R32, HEADS, HS, LAYERS = 8, 16, 32, 8, 16, 2
RH = -(-N_REL // P)

EC = -(-N_EDGES // P)
EG = 13
EI = EC // (2 * EG)
assert EC == 2 * EG * EI

GC = 8
NCH = -(-((N_EDGES + NT * (P - 1)) // P + 1) // (2 * GC)) * 2 * GC
IT = NCH // (2 * GC)
NSLOT = NCH * P
RD, RS = 5, 3
BIG = float(2.0 ** 100)
EPS = 1e-5


class Phase:

    def __init__(self, nc, name):
        self.nc, self.name, self.ctx, self.sems = nc, name, ExitStack(), []

    def sb(self, name, shape, dt=F32):
        return self.ctx.enter_context(self.nc.sbuf_tensor(f"{self.name}_{name}", shape, dt))

    def ps(self, name, shape, dt=F32):
        return self.ctx.enter_context(self.nc.psum_tensor(f"{self.name}_{name}", shape, dt))

    def sem(self, name):
        s = self.nc.alloc_semaphore(f"{self.name}_{name}")
        self.sems.append(s)
        return s

    def __enter__(self):
        return self

    def __exit__(self, *exc):
        if exc[0] is None:
            self.nc.clear_and_free_semaphores(self.sems)
            self.nc.all_engine_barrier()
        self.ctx.close()
        return False


class Chain:

    def __init__(self, eng, sem):
        self.eng, self.sem, self.n = eng, sem, 0

    def link(self, ins):
        self.n += 1
        ins.then_inc(self.sem, 1)
        self.eng.wait_ge(self.sem, self.n)


def each(eng, n):
    def run(body):
        body(0)
        with eng.Fori(1, n) as i:
            body(i)
    return run


def later(count):
    return not (isinstance(count, int) and count == 0)


def load_tiles(nc, eng_type, tile_of, g, n):
    _, tiles = nc.values_load_multi_w_load_instructions(
        tile_of[0:1, bass.ds(g * GC, n)], engines=[eng_type], min_val=0, max_val=NT - 1,
        skip_runtime_bounds_check_because="a count of tiles that start at the chunk or before, less one")
    return tiles


def wide(ap, n):
    return ap.unsqueeze(2).broadcast_to([ap.shape[0], ap.shape[1], n])


def over(ap, n):
    return ap.unsqueeze(1).broadcast_to([ap.shape[0], n, ap.shape[1]])


def phase_constants(nc, S, x, node_type):
    with Phase(nc, "const") as ph:
        s_iota, s_ident, s_load, s_dve = (ph.sem(n) for n in ("iota", "ident", "load", "dve"))
        with nc.Block() as block:

            @block.gpsimd
            def _(pool):
                nc.gpsimd.iota(S.iota_row[:], [[1, P]], base=0, channel_multiplier=0,
                               allow_small_or_imprecise_dtypes=True).then_inc(s_iota, 1)
                nc.gpsimd.iota(S.iota_part[:], [[1, 1]], base=0, channel_multiplier=1,
                               allow_small_or_imprecise_dtypes=True).then_inc(s_iota, 1)

            @block.sync
            def _(sp):
                sp.dma_start(S.x[:], x.rearrange("(a p) d -> p a d", p=P)).then_inc(s_load, 16)
                sp.wait_ge(s_load, 16)

            @block.vector
            def _(dve):
                ch = Chain(dve, s_dve)
                dve.wait_ge(s_iota, 2)
                nc.vector.tensor_scalar(S.ident[:], S.iota_row[:], S.iota_part[:, 0:1], None, ALU.is_equal)
                nc.vector.tensor_scalar(S.before[:], S.iota_row[:], S.iota_part[:, 0:1], None, ALU.is_gt)
                nc.vector.memset(S.ones[:], 1.0)
                for j in range(4):
                    nc.vector.tensor_scalar(S.ident4_bf[:, j, :], S.iota_row[:], S.iota_part[:, 0:1], None,
                                            ALU.is_equal)
                nc.vector.memset(S.eps[:], EPS).then_inc(s_ident, 1)
                sel = ph.sb("sel", [24, 3, HEADS])
                ch.link(nc.vector.tensor_scalar(sel[:], S.iota_row[0:24, 0:24].rearrange("p (k h) -> p k h", k=3),
                                                S.iota_part[0:24, 0:1], None, ALU.is_equal))
                hit = ph.sb("hit", [24, HEADS])
                ch.link(nc.vector.tensor_reduce(hit[:], sel[:].rearrange("p k h -> p h k"), AX_X, ALU.add))
                ch.link(nc.vector.tensor_copy(S.sel8[:], wide(hit[:], P)))
                ch.link(nc.vector.memset(S.sel1[:], 1.0))


def phase_edges(nc, S, T):
    W = EG * P
    with Phase(nc, "edge") as ph:
        dual = ph.sb("dual", [P, RH, 2 * D])
        conv_w = ph.sb("conv_w", [P, 2 * D])
        conv_b = ph.sb("conv_b", [P, 1])
        logit = ph.sb("logit", [P, RH])
        scaled = ph.sb("scaled", [P, RH])
        table = ph.sb("table", [P, RH])
        rel_row = ph.sb("rel_row", [P, 2, W], I32)
        low_row = ph.sb("low_row", [P, 2, W], I32)
        hot_low = ph.sb("hot_low", [P, 2, W])
        hot_high = ph.sb("hot_high", [P, EG, RH])
        picked = ph.sb("picked", [P, EG, RH])
        hot_b = ph.sb("hot_b", [P, 2, EG, P], BF16)
        hot_a = ph.sb("hot_a", [P, 2, EG, NT], BF16)
        zeros = ph.sb("zeros", [P, P], BF16)
        ps_rel = ph.ps("rel", [P, 2, 512])
        ps_deg = ph.ps("deg", [P, 512])
        s_in, s_dve, s_zero, s_deg = (ph.sem(n) for n in ("in", "dve", "zero", "deg"))
        s_row = [ph.sem(f"row{k}") for k in range(2)]
        s_low = [ph.sem(f"low{k}") for k in range(2)]
        s_hot = [ph.sem(f"hot{k}") for k in range(2)]
        s_rel = [ph.sem(f"rel{k}") for k in range(2)]
        s_hots = [ph.sem(f"hots{k}") for k in range(2)]
        s_cnt = [ph.sem(f"cnt{k}") for k in range(2)]
        s_out = [ph.sem(f"out{k}") for k in range(2)]
        s_pick = ph.sem("pick")
        with nc.Block() as block:

            @block.sync
            def _(sp):
                full = (RH - 1) * P
                sp.dma_start(dual[:, 0:RH - 1, :], T["dual_layer"][0:full, :].rearrange("(h p) d -> p h d", p=P)).then_inc(s_in, 16)
                sp.wait_ge(s_zero, 1)
                sp.dma_start(dual[0:N_REL - full, RH - 1, :], T["dual_layer"][full:N_REL, :]).then_inc(s_in, 16)
                sp.dma_start(conv_w[:], T["conv_w"].rearrange("d o -> (o d)").partition_broadcast(P)).then_inc(s_in, 16)
                sp.dma_start(conv_b[:], T["conv_b"].partition_broadcast(P)).then_inc(s_in, 16)
                for k, name in enumerate(("src_key", "dst_key", "src_val", "dst_val", "rel", "type32", "type8")):
                    sp.dma_start(S.raw[:, k, :], T[name]).then_inc(s_in, 16)
                sp.dma_start(S.weight[:], T["weight"]).then_inc(s_in, 16)
                @each(sp, EI)
                def _(i):
                    for k in range(2):
                        if later(i):
                            sp.wait_ge(s_low[k], i)
                        sp.dma_start(rel_row[:, k, :], T["rel_flat"][bass.ds((i * 2 + k) * W, W)].partition_broadcast(P)).then_inc(s_row[k], 16)

            @block.vector
            def _(dve):
                ch = Chain(dve, s_dve)
                nc.vector.memset(zeros[:], 0.0)
                nc.vector.memset(dual[:, RH - 1, :], 0.0).then_inc(s_zero, 1)
                dve.wait_ge(s_in, 12 * 16)
                ch.link(nc.vector.tensor_tensor(dual[:], dual[:], over(conv_w[:], RH), ALU.mult))
                ch.link(nc.vector.tensor_reduce(logit[:], dual[:], AX_X, ALU.add))
                ch.link(nc.vector.tensor_scalar(logit[:], logit[:], conv_b[:, 0:1], None, ALU.add))
                ch.link(nc.vector.tensor_scalar(scaled[:], logit[:], 0.01, None, ALU.mult))
                ch.link(nc.vector.tensor_tensor(table[:], logit[:], scaled[:], ALU.max))
                for key, tile, row in ((0, S.src_a, S.src_b), (1, S.dst_a, S.dst_b)):
                    ch.link(nc.vector.tensor_scalar(S.tmp_i[:], S.raw[:, key, :], 7, None, ALU.logical_shift_right))
                    ch.link(nc.vector.tensor_copy(tile[:], S.tmp_i[:]))
                    ch.link(nc.vector.tensor_scalar(S.tmp_i[:], S.raw[:, key, :], P - 1, None, ALU.bitwise_and))
                    ch.link(nc.vector.tensor_scalar(S.tmp_f[:], tile[:], float(NT), -1000.0, ALU.is_ge, ALU.mult))
                    ch.link(nc.vector.tensor_tensor(row[:], S.tmp_f[:], S.tmp_i[:], ALU.add))
                ch.link(nc.vector.tensor_scalar(S.tmp_i[:], S.raw[:, 4, :], 7, None, ALU.logical_shift_right))
                ch.link(nc.vector.tensor_copy(S.rel_high[:], S.tmp_i[:]))
                ch.link(nc.vector.scalar_tensor_tensor(out=S.row32[:], in0=S.raw[:, 2, :], scalar=float(R32),
                                                       in1=S.raw[:, 5, :], op0=ALU.mult, op1=ALU.add))
                ch.link(nc.vector.scalar_tensor_tensor(out=S.row8[:], in0=S.raw[:, 2, :], scalar=float(R8),
                                                       in1=S.raw[:, 6, :], op0=ALU.mult, op1=ALU.add))
                @each(dve, EI)
                def _(i):
                    for k in range(2):
                        cols = bass.ds((i * 2 + k) * EG, EG)
                        dve.wait_ge(s_row[k], (i + 1) * 16)
                        nc.vector.tensor_scalar(low_row[:, k, :], rel_row[:, k, :], P - 1, None, ALU.bitwise_and).then_inc(s_low[k], 1)
                        dve.wait_ge(s_low[k], i + 1)
                        if later(i):
                            dve.wait_ge(s_rel[k], i)
                        nc.vector.tensor_scalar(hot_low[:, k, :], low_row[:, k, :], S.iota_part[:, 0:1], None,
                                                ALU.is_equal).then_inc(s_hot[k], 1)
                        if later(i):
                            dve.wait_ge(s_cnt[k], i)
                        nc.vector.tensor_tensor(hot_b[:, k], over(S.iota_row[:], EG), wide(S.dst_b[:, cols], P), ALU.is_equal)
                        nc.vector.tensor_tensor(hot_a[:, k], over(S.iota_row[:, 0:NT], EG), wide(S.dst_a[:, cols], NT),
                                                ALU.is_equal).then_inc(s_hots[k], 1)
                        nc.vector.tensor_tensor(hot_high[:], over(S.iota_row[:, 0:RH], EG), wide(S.rel_high[:, cols], RH),
                                                ALU.is_equal).then_inc(s_pick, 1)
                        dve.wait_ge(s_pick, i * 4 + 2 * k + 1)
                        dve.wait_ge(s_rel[k], i + 1)
                        nc.vector.tensor_tensor(picked[:], ps_rel[:, k, 0:EG * RH].rearrange("p (c h) -> p c h", h=RH),
                                                hot_high[:], ALU.mult).then_inc(s_pick, 1)
                        dve.wait_ge(s_pick, i * 4 + 2 * k + 2)
                        nc.vector.tensor_reduce(S.score[:, cols], picked[:], AX_X, ALU.add).then_inc(s_out[k], 1)
                dve.wait_ge(s_out[1], EI)
                dve.wait_ge(s_deg, 1)
                ch.link(nc.vector.tensor_scalar(S.dinv[:], ps_deg[:, 0:NT], 1.0, None, ALU.add))

            @block.scalar
            def _(act):
                act.wait_ge(s_dve, 20)
                nc.scalar.activation(S.dinv[:], S.dinv[:], ACT.Sqrt).then_inc(s_zero, 1)

            @block.tensor
            def _(pe):
                pe.wait_ge(s_zero, 1)
                nc.tensor.matmul(ps_deg[:, 0:NT], zeros[:], zeros[:, 0:NT], start=True, stop=False, skip_group_check=True)
                @each(pe, EI)
                def _(i):
                    for k in range(2):
                        pe.wait_ge(s_hot[k], i + 1)
                        if later(i):
                            pe.wait_ge(s_out[k], i)
                        for c in range(EG):
                            mm = nc.tensor.matmul(ps_rel[:, k, c * RH:(c + 1) * RH], hot_low[:, k, c * P:(c + 1) * P], table[:],
                                                  start=True, stop=True)
                        mm.then_inc(s_rel[k], 1)
                        pe.wait_ge(s_hots[k], i + 1)
                        for c in range(EG):
                            mm = nc.tensor.matmul(ps_deg[:, 0:NT], hot_b[:, k, c, :], hot_a[:, k, c, :],
                                                  start=False, stop=False, skip_group_check=True)
                        mm.then_inc(s_cnt[k], 1)
                nc.tensor.matmul(ps_deg[:, 0:NT], zeros[:], zeros[:, 0:NT], start=False, stop=True, skip_group_check=True).then_inc(s_deg, 1)


def phase_rank(nc, S, name, tile, slot, tile_of):
    NB = NT + 1
    with Phase(nc, name) as ph:
        mask = ph.sb("mask", [P, EC])
        zeros = ph.sb("zeros", [P, EC])
        rank = ph.sb("rank", [P, EC])
        place = ph.sb("place", [P, EC])
        count = ph.sb("count", [P, NB])
        chunks_i = ph.sb("chunks_i", [P, NB], I32)
        chunks = ph.sb("chunks", [P, NB])
        last = ph.sb("last", [P, NB])
        start = ph.sb("start", [P, NB])
        tiles_i = ph.sb("tiles_i", [NT, 1], I32)
        tiles = ph.sb("tiles", [NT, 1])
        first = ph.sb("first", [NT, 1])
        chunk_no = ph.sb("chunk_no", [NT, NCH])
        past = ph.sb("past", [NT, NCH])
        ps = ph.ps("ps", [P, 512])
        ps_t = ph.ps("ps_t", [P, 512])
        ps_c = ph.ps("ps_c", [1, 2, 512])
        s_dve, s_pe, s_it, s_io = (ph.sem(n) for n in ("dve", "pe", "it", "io"))
        with nc.Block() as block:

            @block.gpsimd
            def _(pool):
                nc.gpsimd.iota(chunk_no[:], [[1, NCH]], base=0, channel_multiplier=0,
                               allow_small_or_imprecise_dtypes=True).then_inc(s_io, 1)

            @block.vector
            def _(dve):
                ch = Chain(dve, s_dve)
                nc.vector.memset(zeros[:], 0.0)
                ch.link(nc.vector.memset(place[:], 0.0))
                @each(dve, NB)
                def _(t):
                    if later(t):
                        dve.wait_ge(s_it, t)
                    nc.vector.tensor_scalar(mask[:], tile[:], S.iota_row[:, bass.ds(t, 1)], 0.0, ALU.is_equal, ALU.add,
                                            accum_out=count[:, bass.ds(t, 1)]).then_inc(s_it, 1)
                dve.wait_ge(s_pe, 1)
                for n_i, n, tot in ((chunks_i, chunks, ps[:, 64:64 + NB]), (tiles_i, tiles, ps_t[0:NT, 0:1])):
                    ch.link(nc.vector.tensor_scalar(n_i[:], tot, float(P - 1), None, ALU.add))
                    ch.link(nc.vector.tensor_scalar(n_i[:], n_i[:], 7, None, ALU.logical_shift_right))
                    ch.link(nc.vector.tensor_copy(n[:], n_i[:]))
                ch.link(nc.vector.tensor_tensor_scan(last[:], chunks[:], zeros[:, 0:NB], 0.0, ALU.add, ALU.add))
                ch.link(nc.vector.tensor_tensor(start[:], last[:], chunks[:], ALU.subtract))
                ch.link(nc.vector.tensor_scalar(start[:], start[:], float(P), -1.0, ALU.mult, ALU.add))
                ch.link(nc.vector.tensor_tensor(start[:], start[:], ps[:, 0:NB], ALU.add))
                @each(dve, NB)
                def _(t):
                    if later(t * 4 + NB):
                        dve.wait_ge(s_it, t * 4 + NB)
                    nc.vector.tensor_scalar(mask[:], tile[:], S.iota_row[:, bass.ds(t, 1)], None, ALU.is_equal).then_inc(s_it, 1)
                    dve.wait_ge(s_it, t * 4 + NB + 1)
                    nc.vector.tensor_tensor_scan(rank[:], mask[:], zeros[:], start[:, bass.ds(t, 1)], ALU.add, ALU.add).then_inc(s_it, 1)
                    dve.wait_ge(s_it, t * 4 + NB + 2)
                    nc.vector.tensor_tensor(rank[:], rank[:], mask[:], ALU.mult).then_inc(s_it, 1)
                    dve.wait_ge(s_it, t * 4 + NB + 3)
                    nc.vector.tensor_tensor(place[:], place[:], rank[:], ALU.add).then_inc(s_it, 1)
                dve.wait_ge(s_it, NB * 5)
                ch.link(nc.vector.tensor_copy(slot[:], place[:]))
                ch.link(nc.vector.tensor_scalar(S.tmp_i[:], slot[:], 7, None, ALU.logical_shift_right))
                ch.link(nc.vector.tensor_scalar(slot[:], slot[:], P - 1, None, ALU.bitwise_and))
                ch.link(nc.vector.scalar_tensor_tensor(out=slot[:], in0=slot[:], scalar=float(NCH), in1=S.tmp_i[:],
                                                       op0=ALU.mult, op1=ALU.add))
                dve.wait_ge(s_pe, 2)
                ch.link(nc.vector.tensor_copy(first[:], ps_t[0:NT, 1:2]))
                dve.wait_ge(s_io, 1)
                ch.link(nc.vector.tensor_scalar(past[:], chunk_no[:], first[:, 0:1], None, ALU.is_ge))
                dve.wait_ge(s_pe, 3)
                ch.link(nc.vector.tensor_scalar(tile_of[:].rearrange("p (h c) -> p h c", h=2),
                                                ps_c[0:1, :, 0:NCH // 2], -1.0, None, ALU.add))

            @block.tensor
            def _(pe):
                pe.wait_ge(s_it, NB)
                nc.tensor.matmul(ps[:, 0:NB], S.before[:], count[:], start=True, stop=True)
                nc.tensor.matmul(ps[:, 64:64 + NB], S.ones[:], count[:], start=True, stop=True)
                nc.tensor.matmul(ps_t[0:NT, 0:1], count[:, 0:NT], S.ones[:, 0:1], start=True, stop=True).then_inc(s_pe, 1)
                pe.wait_ge(s_dve, 7)
                nc.tensor.matmul(ps_t[0:NT, 1:2], S.before[0:NT, 0:NT], tiles[:], start=True, stop=True).then_inc(s_pe, 1)
                pe.wait_ge(s_dve, 17)
                for h in range(2):
                    mm = nc.tensor.matmul(ps_c[0:1, h, 0:NCH // 2], S.ones[0:NT, 0:1], past[:, h * NCH // 2:(h + 1) * NCH // 2],
                                          start=True, stop=True)
                mm.then_inc(s_pe, 1)


def phase_scatter(nc, S, name, slot, fields, words, records, kept):
    with Phase(nc, name) as ph:
        stage = ph.sb("stage", [P, 2, EG, words], I32)
        place = ph.sb("place", [P, 2, EG], U32)
        s_fill, s_init, s_go = ph.sem("fill"), ph.sem("init"), ph.sem("go")
        s_stage = [ph.sem(f"stage{k}") for k in range(2)]
        s_scat = [ph.sem(f"scat{k}") for k in range(2)]
        with nc.Block() as block:

            @block.vector
            def _(dve):
                nc.vector.memset(kept[:], 0).then_inc(s_fill, 1)
                dve.wait_ge(s_fill, 1)
                nc.vector.memset(kept[:, :, 1:2].bitcast(F32), -1.0).then_inc(s_fill, 1)
                @each(dve, EI)
                def _(i):
                    for k in range(2):
                        cols = bass.ds((i * 2 + k) * EG, EG)
                        if later(i * (EG * 16)):
                            dve.wait_ge(s_scat[k], i * (EG * 16))
                        for f, field in enumerate(fields):
                            nc.vector.tensor_copy(stage[:, k, :, f], field(cols))
                        nc.vector.tensor_copy(place[:, k, :], slot[:, cols]).then_inc(s_stage[k], 1)

            @block.gpsimd
            def _(pool):
                pool.wait_ge(s_init, 16)
                @each(pool, EI)
                def _(i):
                    for k in range(2):
                        pool.wait_ge(s_stage[k], i + 1)
                        pool.sem_inc(s_go, 1)
                        for c in range(EG):
                            pool.indirect_dma_start(records, bass.IndirectOffsetOnAxis(ap=place[:, k, c:c + 1], axis=0),
                                                    stage[:, k, c, :], None).then_inc(s_scat[k], 16)

            @block.sync
            def _(sp):
                sp.wait_ge(s_fill, 2)
                whole = records.rearrange("(p c) w -> p (c w)", p=P)
                sp.dma_start(whole, kept[:].rearrange("p c w -> p (c w)")).then_inc(s_init, 16)
                sp.wait_ge(s_scat[0], EI * EG * 16)
                sp.wait_ge(s_scat[1], EI * EG * 16)
                sp.dma_start(kept[:].rearrange("p c w -> p (c w)"), whole).then_inc(s_init, 16)
                sp.wait_ge(s_init, 32)


def phase_max(nc, S, name, H, records, tile_of, table=None, field=0, q=None):
    HG = H * 3
    CPS = GC // H
    SLOTS = GC // CPS
    with Phase(nc, name) as ph:
        hot = ph.sb("hot", [P, 2, GC, P])
        miss = ph.sb("miss", [P, 2, GC, P], BF16)
        part = ph.sb("part", [P, 2, GC, HG], BF16)
        rest = ph.sb("rest", [P, GC, H])
        rest2 = ph.sb("rest2", [P, GC, H])
        parts_t = ph.sb("parts_t", [HG, 2, GC * P], BF16)
        top = ph.sb("top", [P, GC, H])
        ps_m = ph.ps("m", [P, 2, 1024])
        ps_p = ph.ps("p", [HG, GC * P], BF16)
        s_hot, s_miss, s_score, s_part, s_pt = ([ph.sem(f"{n}{k}") for k in range(2)]
                                                for n in ("hot", "miss", "score", "part", "pt"))
        s_cp, s_up, s_ch, s_init = (ph.sem(n) for n in ("cp", "up", "ch", "init"))
        s_full = [[ph.sem(f"full{k}{j}") for j in range(2)] for k in range(2)]
        s_read = [ph.sem(f"read{j}") for j in range(2)]
        per = max(1, SLOTS // 2)

        def slot(m, k):
            return m % 2 if SLOTS > 1 else k

        def products_done(eng, k, i):
            if later(i * per):
                eng.wait_ge(s_full[k][slot(SLOTS - 1, k)], i * per)
        if table is not None:
            ring = ph.sb("ring", [P, 2, GC, D])
            index = ph.sb("index", [P, 2, GC], U32)
            hot_t = ph.sb("hot_t", [P, 2, GC, P])
            ps_t = ph.ps("t", [P, 512])
            ps_q = ph.ps("q", [P, 1024])
            s_gath = [ph.sem(f"gath{k}") for k in range(2)]
            s_ix, s_go, s_tr, s_tc, s_q, s_prod = (ph.sem(n) for n in ("ix", "go", "tr", "tc", "q", "prod"))
        fields = records[:].bitcast(F32)
        with nc.Block() as block:

            if table is not None:
                @block.gpsimd
                def _(pool):
                    @each(pool, IT)
                    def _(i):
                        for k in range(2):
                            if later(i):
                                pool.wait_ge(s_score[k], i)
                            nc.gpsimd.tensor_copy(index[:, k, :], records[:, bass.ds((i * 2 + k) * GC, GC), field]).then_inc(s_ix, 1)
                            pool.wait_ge(s_ix, i * 2 + k + 1)
                            pool.sem_inc(s_go, 1)
                            for c in range(GC):
                                pool.indirect_dma_start(ring[:, k, c, :], None, table,
                                                        bass.IndirectOffsetOnAxis(ap=index[:, k, c:c + 1], axis=0)).then_inc(s_gath[k], 16)

            @block.vector
            def _(dve):
                nc.vector.memset(S.mx[:], -BIG).then_inc(s_init, 1)
                dve.wait_ge(s_init, 1)
                @each(dve, IT)
                def _(i):
                    tiles = load_tiles(nc, mybir.EngineType.DVE, tile_of, i * 2, 2 * GC)
                    for k in range(2):
                        g = i * 2 + k
                        cols = bass.ds(g * GC, GC)
                        products_done(dve, k, i)
                        if later(i):
                            dve.wait_ge(s_miss[k], i)
                        nc.vector.tensor_tensor(hot[:, k], over(S.iota_row[:], GC), wide(fields[:, cols, 1], P),
                                                ALU.is_equal).then_inc(s_hot[k], 1)
                        if table is None:
                            nc.vector.tensor_copy(S.score_of[:, cols, 0:1], fields[:, cols, 2:3]).then_inc(s_score[k], 1)
                        else:
                            dve.wait_ge(s_gath[k], (i + 1) * (GC * 16))
                            dve.wait_ge(s_q, g + 1)
                            nc.vector.tensor_tensor(ring[:, k], ring[:, k], ps_q[:].rearrange("p (c d) -> p c d", d=D),
                                                    ALU.mult).then_inc(s_prod, 1)
                            dve.wait_ge(s_prod, g + 1)
                            nc.vector.tensor_reduce(S.score_of[:, cols, :].rearrange("p c h -> p (c h)"),
                                                    ring[:, k].rearrange("p c (h d) -> p (c h) d", d=HS), AX_X,
                                                    ALU.add).then_inc(s_score[k], 1)
                        sc = S.score_of[:, cols, 0:H]
                        dve.wait_ge(s_score[k], i + 1)
                        nc.vector.tensor_scalar(part[:, k, :, 0:H], sc, 1.0, None, ALU.mult).then_inc(s_ch, 1)
                        dve.wait_ge(s_ch, g * 4 + 1)
                        nc.vector.tensor_tensor(rest[:], sc, part[:, k, :, 0:H], ALU.subtract).then_inc(s_ch, 1)
                        dve.wait_ge(s_ch, g * 4 + 2)
                        nc.vector.tensor_copy(part[:, k, :, H:2 * H], rest[:]).then_inc(s_ch, 1)
                        dve.wait_ge(s_ch, g * 4 + 3)
                        nc.vector.tensor_tensor(rest2[:], rest[:], part[:, k, :, H:2 * H], ALU.subtract).then_inc(s_ch, 1)
                        dve.wait_ge(s_ch, g * 4 + 4)
                        nc.vector.tensor_copy(part[:, k, :, 2 * H:3 * H], rest2[:]).then_inc(s_part[k], 1)
                        for m in range(SLOTS):
                            j = slot(m, k)
                            dve.wait_ge(s_full[k][j], i * per + m // 2 + 1)
                            out = top[:, m * CPS:(m + 1) * CPS, :].rearrange("p c h -> p (c h)")
                            nc.vector.tensor_reduce(out, ps_m[:, j, :].rearrange("p (h e) -> p h e", e=P), AX_X,
                                                    ALU.max).then_inc(s_read[j], 1)
                        if SLOTS > 1:
                            dve.wait_ge(s_read[0], (g + 1) * per)
                            dve.wait_ge(s_read[1], (g + 1) * per)
                        else:
                            dve.wait_ge(s_read[k], i + 1)
                        for c in range(GC):
                            mx = S.mx[:, bass.ds(tiles[k * GC + c], 1), 0:H]
                            nc.vector.tensor_tensor(mx, mx, top[:, c:c + 1, :], ALU.max).then_inc(s_up, 1)
                            dve.wait_ge(s_up, g * GC + c + 1)

            @block.scalar
            def _(act):
                @each(act, IT)
                def _(i):
                    for k in range(2):
                        g = i * 2 + k
                        act.wait_ge(s_hot[k], i + 1)
                        products_done(act, k, i)
                        nc.scalar.activation(miss[:, k], hot[:, k], ACT.Copy, bias=-BIG, scale=BIG).then_inc(s_miss[k], 1)
                        if table is not None:
                            for h in range(2):
                                act.wait_ge(s_tr, g * 2 + h + 1)
                                nc.scalar.copy(hot_t[:, k, h * 4:h * 4 + 4, :].rearrange("p c e -> p (c e)"), ps_t[:]).then_inc(s_tc, 1)
                        act.wait_ge(s_pt[k], i + 1)
                        nc.scalar.copy(parts_t[:, k, :], ps_p[:]).then_inc(s_cp, 1)

            @block.tensor
            def _(pe):
                @each(pe, IT)
                def _(i):
                    if table is not None:
                        tiles = load_tiles(nc, mybir.EngineType.PE, tile_of, i * 2, 2 * GC)
                    for k in range(2):
                        g = i * 2 + k
                        pe.wait_ge(s_hot[k], i + 1)
                        if table is not None:
                            for h in range(2):
                                if later(g * 2 + h):
                                    pe.wait_ge(s_tc, g * 2 + h)
                                for c in range(4):
                                    mm = nc.tensor.transpose(ps_t[:, c * P:(c + 1) * P], hot[:, k, h * 4 + c, :], S.ident[:])
                                mm.then_inc(s_tr, 1)
                            pe.wait_ge(s_tc, g * 2 + 2)
                            if later(g):
                                pe.wait_ge(s_prod, g)
                            for c in range(GC):
                                mm = nc.tensor.matmul(ps_q[:, c * P:(c + 1) * P], hot_t[:, k, c, :],
                                                      q[:, bass.ds(tiles[k * GC + c], 1), :].rearrange("p a d -> p (a d)"),
                                                      start=True, stop=True)
                            mm.then_inc(s_q, 1)
                        pe.wait_ge(s_part[k], i + 1)
                        if later(g):
                            pe.wait_ge(s_cp, g)
                        for c in range(GC):
                            mm = nc.tensor.transpose(ps_p[:, c * P:(c + 1) * P], part[:, k, c, :], S.ident4_bf[:, 0, :])
                        mm.then_inc(s_pt[k], 1)
                        pe.wait_ge(s_cp, g + 1)
                        pe.wait_ge(s_miss[k], i + 1)
                        for m in range(SLOTS):
                            j = slot(m, k)
                            if later((g * per + m // 2) if SLOTS > 1 else i):
                                pe.wait_ge(s_read[j], (g * per + m // 2) if SLOTS > 1 else i)
                            for b in range(2):
                                bank = ps_m[:, j, b * 512:(b + 1) * 512]
                                if H == HEADS:
                                    nc.tensor.matmul(bank, miss[:, k, m, :], S.ident4_bf[:].rearrange("p a e -> p (a e)"),
                                                     start=True, stop=False, skip_group_check=True)
                                    for h in range(4):
                                        mm = nc.tensor.matmul(bank[:, h * P:(h + 1) * P], S.sel8[:, b * 4 + h, :],
                                                              parts_t[:, k, m * P:(m + 1) * P], start=False, stop=(h == 3),
                                                              skip_group_check=True)
                                else:
                                    nc.tensor.matmul(bank, S.sel1[:], parts_t[:, k, b * 512:(b + 1) * 512], start=True, stop=False,
                                                     skip_group_check=True)
                                    for c in range(4):
                                        mm = nc.tensor.matmul(bank[:, c * P:(c + 1) * P], miss[:, k, b * 4 + c, :], S.ident4_bf[:, 0, :],
                                                              start=False, stop=(c == 3), skip_group_check=True)
                            mm.then_inc(s_full[k][j], 1)


def phase_sum(nc, S, name, H, records, tile_of, table, field, weight=False):
    W = D + H
    with Phase(nc, name) as ph:
        ring = ph.sb("ring", [P, 2, GC, D])
        index = ph.sb("index", [P, 2, GC], U32)
        hot = ph.sb("hot", [P, 2, GC, P])
        ps_o = ph.ps("o", [P, 2, 2, 2, 256])
        s_gath, s_hot, s_val = ([ph.sem(f"{n}{k}") for k in range(2)] for n in ("gath", "hot", "val"))
        s_full = [[ph.sem(f"full{k}{h}") for h in range(2)] for k in range(2)]
        s_add = [ph.sem(f"add{h}") for h in range(2)]
        s_ix, s_init, s_go = ph.sem("ix"), ph.sem("init"), ph.sem("go")
        if H:
            hot_t = ph.sb("hot_t", [P, 2, GC, P])
            dist = ph.sb("dist", [P, 2, GC, H])
            wt = ph.sb("wt", [P, 2, GC, H])
            ps_t = ph.ps("t", [P, 512])
            ps_e = ph.ps("e", [P, 512])
            s_tr, s_tc, s_me, s_dist, s_exp = (ph.sem(n) for n in ("tr", "tc", "me", "dist", "exp"))
        fields = records[:].bitcast(F32)
        with nc.Block() as block:

            @block.gpsimd
            def _(pool):
                @each(pool, IT)
                def _(i):
                    for k in range(2):
                        if later(i):
                            pool.wait_ge(s_full[k][1], i)
                        nc.gpsimd.tensor_copy(index[:, k, :], records[:, bass.ds((i * 2 + k) * GC, GC), field]).then_inc(s_ix, 1)
                        pool.wait_ge(s_ix, i * 2 + k + 1)
                        pool.sem_inc(s_go, 1)
                        for c in range(GC):
                            pool.indirect_dma_start(ring[:, k, c, :], None, table,
                                                    bass.IndirectOffsetOnAxis(ap=index[:, k, c:c + 1], axis=0)).then_inc(s_gath[k], 16)

            @block.vector
            def _(dve):
                nc.vector.memset(S.acc[:], 0.0).then_inc(s_init, 1)
                dve.wait_ge(s_init, 1)
                @each(dve, IT)
                def _(i):
                    tiles = load_tiles(nc, mybir.EngineType.DVE, tile_of, i * 2, 2 * GC)
                    for k in range(2):
                        g = i * 2 + k
                        cols = bass.ds(g * GC, GC)
                        if later(i):
                            dve.wait_ge(s_full[k][1], i)
                        nc.vector.tensor_tensor(hot[:, k], over(S.iota_row[:], GC), wide(fields[:, cols, 1], P),
                                                ALU.is_equal).then_inc(s_hot[k], 1)
                        if H:
                            dve.wait_ge(s_me, g + 1)
                            nc.vector.tensor_tensor(dist[:, k], S.score_of[:, cols, 0:H],
                                                    ps_e[:, 0:GC * H].rearrange("p (c h) -> p c h", h=H),
                                                    ALU.subtract).then_inc(s_dist, 1)
                            dve.wait_ge(s_exp, g + 1)
                        dve.wait_ge(s_gath[k], (i + 1) * (GC * 16))
                        if H:
                            nc.vector.tensor_tensor(ring[:, k].rearrange("p c (h d) -> p (c h) d", h=H),
                                                    ring[:, k].rearrange("p c (h d) -> p (c h) d", h=H),
                                                    wide(wt[:, k].rearrange("p c h -> p (c h)"), D // H),
                                                    ALU.mult).then_inc(s_val[k], 1)
                        elif weight:
                            nc.vector.tensor_tensor(ring[:, k], ring[:, k], wide(fields[:, cols, 2], D), ALU.mult).then_inc(s_val[k], 1)
                        for h in range(2):
                            dve.wait_ge(s_full[k][h], i + 1)
                            for c in range(4):
                                a = S.acc[:, bass.ds(tiles[k * GC + h * 4 + c], 1), 0:W]
                                nc.vector.tensor_tensor(a, a, ps_o[:, h, c // 2, c % 2:c % 2 + 1, 0:W], ALU.add).then_inc(s_add[h], 1)
                                dve.wait_ge(s_add[h], g * 4 + c + 1)

            @block.scalar
            def _(act):
                if H:
                    @each(act, IT)
                    def _(i):
                        for k in range(2):
                            g = i * 2 + k
                            if later(i):
                                act.wait_ge(s_full[k][1], i)
                            for h in range(2):
                                act.wait_ge(s_tr, g * 2 + h + 1)
                                nc.scalar.copy(hot_t[:, k, h * 4:h * 4 + 4, :].rearrange("p c e -> p (c e)"), ps_t[:]).then_inc(s_tc, 1)
                            act.wait_ge(s_dist, g + 1)
                            nc.scalar.activation(wt[:, k], dist[:, k], ACT.Exp).then_inc(s_exp, 1)

            @block.tensor
            def _(pe):
                @each(pe, IT)
                def _(i):
                    if H:
                        tiles = load_tiles(nc, mybir.EngineType.PE, tile_of, i * 2, 2 * GC)
                    for k in range(2):
                        g = i * 2 + k
                        pe.wait_ge(s_hot[k], i + 1)
                        if H:
                            for h in range(2):
                                if later(g * 2 + h):
                                    pe.wait_ge(s_tc, g * 2 + h)
                                for c in range(4):
                                    mm = nc.tensor.transpose(ps_t[:, c * P:(c + 1) * P], hot[:, k, h * 4 + c, :], S.ident[:])
                                mm.then_inc(s_tr, 1)
                            pe.wait_ge(s_tc, g * 2 + 2)
                            if later(g):
                                pe.wait_ge(s_dist, g)
                            for c in range(GC):
                                mm = nc.tensor.matmul(ps_e[:, c * H:(c + 1) * H], hot_t[:, k, c, :],
                                                      S.mx[:, bass.ds(tiles[k * GC + c], 1), 0:H].rearrange("p a h -> p (a h)"),
                                                      start=True, stop=True)
                            mm.then_inc(s_me, 1)
                        if H or weight:
                            pe.wait_ge(s_val[k], i + 1)
                        else:
                            pe.wait_ge(s_gath[k], (i + 1) * (GC * 16))
                        for h in range(2):
                            if later(g * 4):
                                pe.wait_ge(s_add[h], g * 4)
                            for c in range(4):
                                o = ps_o[:, h, c // 2, c % 2, :]
                                mm = nc.tensor.matmul(o[:, 0:D], hot[:, k, h * 4 + c, :], ring[:, k, h * 4 + c, :], start=True, stop=True)
                                if H:
                                    mm = nc.tensor.matmul(o[:, D:W], hot[:, k, h * 4 + c, :], wt[:, k, h * 4 + c, :], start=True, stop=True)
                            mm.then_inc(s_full[k][h], 1)


def phase_transpose(nc, S, name, source, target):
    GROUPS = [range(a, min(a + 4, NT)) for a in range(0, NT, 4)]
    with Phase(nc, name) as ph:
        ps = ph.ps("ps", [P, 2, 512])
        s_tr, s_cp = ph.sem("tr"), ph.sem("cp")
        with nc.Block() as block:

            @block.tensor
            def _(pe):
                for g, tiles in enumerate(GROUPS):
                    if g >= 2:
                        pe.wait_ge(s_cp, g - 1)
                    for c, a in enumerate(tiles):
                        mm = nc.tensor.transpose(ps[:, g % 2, c * P:(c + 1) * P], source[:, a, :], S.ident[:])
                    mm.then_inc(s_tr, 1)

            @block.scalar
            def _(act):
                for g, tiles in enumerate(GROUPS):
                    act.wait_ge(s_tr, g + 1)
                    n = len(tiles) * P
                    nc.scalar.copy(target[:, g * 512:g * 512 + n], ps[:, g % 2, 0:n]).then_inc(s_cp, 1)


def phase_expand(nc, S, name, source_t, matrix, table):
    C = matrix.shape[1]
    U, TI, RING = C // 512, 5, 5
    rows = table.rearrange("(a p t) d -> a p (t d)", p=P, a=NT)
    with Phase(nc, name) as ph:
        left = ph.sb("left", [P, TI, P])
        out = ph.sb("out", [P, RING, 512])
        ps = ph.ps("ps", [P, RING, 512])
        s_left = ph.sem("left")
        s_mm, s_ev, s_wr = ([ph.sem(f"{n}{r}") for r in range(RING)] for n in ("mm", "ev", "wr"))

        def evacuate(eng, copy, i, u):
            r, n = u % RING, i * U + u // RING
            eng.wait_ge(s_mm[r], n + 1)
            if later(n * 16):
                eng.wait_ge(s_wr[r], n * 16)
            copy(out[:, r, :], ps[:, r, :]).then_inc(s_ev[r], 1)

        with nc.Block() as block:

            @block.vector
            def _(dve):
                @each(dve, NT // TI)
                def _(i):
                    if later(i * U):
                        dve.wait_ge(s_mm[RING - 1], i * U)
                    nc.vector.tensor_copy(left[:].rearrange("p a n -> p (a n)"),
                                          source_t[:, bass.ds(i * (TI * P), TI * P)]).then_inc(s_left, 1)
                    for u in range(0, TI * U, 2):
                        evacuate(dve, nc.vector.tensor_copy, i, u)

            @block.scalar
            def _(act):
                @each(act, NT // TI)
                def _(i):
                    for u in range(1, TI * U, 2):
                        evacuate(act, nc.scalar.copy, i, u)

            @block.tensor
            def _(pe):
                @each(pe, NT // TI)
                def _(i):
                    pe.wait_ge(s_left, i + 1)
                    for u in range(TI * U):
                        r, n = u % RING, i * U + u // RING
                        if later(n):
                            pe.wait_ge(s_ev[r], n)
                        nc.tensor.matmul(ps[:, r, :], left[:, u // U, :], matrix[:, (u % U) * 512:(u % U + 1) * 512],
                                         start=True, stop=True).then_inc(s_mm[r], 1)

            @block.sync
            def _(sp):
                @each(sp, NT // TI)
                def _(i):
                    for u in range(TI * U):
                        r, n = u % RING, i * U + u // RING
                        sp.wait_ge(s_ev[r], n + 1)
                        sp.dma_start(rows[bass.ds(i * TI + u // U, 1), :, (u % U) * 512:(u % U + 1) * 512].rearrange("a p c -> (a p) c"),
                                     out[:, r, :]).then_inc(s_wr[r], 16)
                for r in range(RING):
                    sp.wait_ge(s_wr[r], (NT // TI) * U * 16)


def phase_typed(nc, S, name, source_t, weights, node_type, outs):
    n_out, HALF = len(outs), R16 // 2
    with Phase(nc, name) as ph:
        w = ph.sb("w", [P, n_out, R16, P])
        types = ph.sb("types", [P, N_PAD], I32)
        only = ph.sb("only", [P, R16, P])
        ps = [ph.ps(f"ps{o}", [P, 512]) for o in range(n_out)]
        s_in, s_ev = ph.sem("in"), ph.sem("ev")
        s_only, s_mm = ([ph.sem(f"{n}{k}") for k in range(2)] for n in ("only", "mm"))
        with nc.Block() as block:

            @block.sync
            def _(sp):
                sp.dma_start(types[:], node_type.partition_broadcast(P)).then_inc(s_in, 16)
                for o, weight in enumerate(weights):
                    sp.dma_start(w[:, o], weight.rearrange("t d o -> d t o")).then_inc(s_in, 16)

            @block.vector
            def _(dve):
                dve.wait_ge(s_in, 16 * (1 + n_out))
                @each(dve, NT)
                def _(a):
                    cols = bass.ds(a * P, P)
                    for k in range(2):
                        if later(a):
                            dve.wait_ge(s_mm[k], a)
                        for t in range(k * HALF, (k + 1) * HALF):
                            ins = nc.vector.scalar_tensor_tensor(out=only[:, t, :], in0=types[:, cols], scalar=float(t),
                                                                 in1=source_t[:, cols], op0=ALU.is_equal, op1=ALU.mult)
                        ins.then_inc(s_only[k], 1)

            @block.tensor
            def _(pe):
                pe.wait_ge(s_in, 16 * (1 + n_out))
                @each(pe, NT)
                def _(a):
                    if later(a * n_out):
                        pe.wait_ge(s_ev, a * n_out)
                    for k in range(2):
                        pe.wait_ge(s_only[k], a + 1)
                        for t in range(k * HALF, (k + 1) * HALF):
                            for o, (_, across, _) in enumerate(outs):
                                left, right = (w[:, o, t, :], only[:, t, :]) if across else (only[:, t, :], w[:, o, t, :])
                                mm = nc.tensor.matmul(ps[o][:, 0:P], left, right, start=(t == 0), stop=(t == R16 - 1))
                        mm.then_inc(s_mm[k], 1)

            @block.scalar
            def _(act):
                @each(act, NT)
                def _(a):
                    act.wait_ge(s_mm[1], a + 1)
                    for o, (target, _, function) in enumerate(outs):
                        nc.scalar.activation(target[:, bass.ds(a * P, P)], ps[o][:, 0:P], function).then_inc(s_ev, 1)


def phase_heads(nc, S, name, matrix, weight, pri=None):
    with Phase(nc, name) as ph:
        scale = ph.sb("scale", [P, R32])
        s_zero, s_in, s_dve = ph.sem("zero"), ph.sem("in"), ph.sem("dve")
        n_in = 16 * HEADS * (1 if pri is None else 2)
        m = matrix[:].rearrange("p (t o) -> p t o", o=P)
        with nc.Block() as block:

            @block.sync
            def _(sp):
                sp.wait_ge(s_zero, 1)
                for h in range(HEADS):
                    at = slice(h * HS, (h + 1) * HS)
                    sp.dma_start(m[at, :, at], weight[h].rearrange("t d o -> d t o")).then_inc(s_in, 16)
                    if pri is not None:
                        sp.dma_start(scale[at, :], pri[h].partition_broadcast(HS)).then_inc(s_in, 16)
                sp.wait_ge(s_in, n_in)

            @block.vector
            def _(dve):
                nc.vector.memset(matrix[:], 0.0).then_inc(s_zero, 1)
                if pri is not None:
                    ch = Chain(dve, s_dve)
                    dve.wait_ge(s_in, n_in)
                    ch.link(nc.vector.tensor_scalar(scale[:], scale[:], float(HS) ** -0.5, None, ALU.mult))
                    ch.link(nc.vector.tensor_tensor(m, m, wide(scale[:], P), ALU.mult))


def phase_scaled_table(nc, S, name, source, target, table):
    with Phase(nc, name) as ph:
        s_dve, s_wr = ph.sem("dve"), ph.sem("wr")
        with nc.Block() as block:

            @block.vector
            def _(dve):
                nc.vector.tensor_tensor(target[:], source[:], wide(S.dinv[:], D), ALU.mult).then_inc(s_dve, 1)

            @block.sync
            def _(sp):
                sp.wait_ge(s_dve, 1)
                sp.dma_start(table.rearrange("(a p) d -> p a d", p=P), target[:]).then_inc(s_wr, 16)
                sp.wait_ge(s_wr, 16)


def phase_gcn_dense(nc, S, source_t, W1, b1, W2, target):
    HB = HID // P
    with Phase(nc, "gcn") as ph:
        w1 = ph.sb("w1", [P, HID])
        w2 = ph.sb("w2", [P, HB, D])
        bias = ph.sb("bias", [P, HB])
        hidden = ph.sb("hidden", [P, HB, P])
        ps_h = ph.ps("h", [P, HB, 512])
        ps_o = ph.ps("o", [P, 512])
        s_in, s_h, s_act, s_o, s_ev = (ph.sem(n) for n in ("in", "h", "act", "o", "ev"))
        with nc.Block() as block:

            @block.sync
            def _(sp):
                sp.dma_start(w1[:], W1).then_inc(s_in, 16)
                sp.dma_start(w2[:], W2.rearrange("(h p) o -> p h o", p=P)).then_inc(s_in, 16)
                for h in range(HB):
                    sp.dma_start(bias[:, h:h + 1], b1[h * P:(h + 1) * P].unsqueeze(1)).then_inc(s_in, 16)

            @block.tensor
            def _(pe):
                pe.wait_ge(s_in, 64)
                @each(pe, NT)
                def _(a):
                    for h in range(HB):
                        if later(a * HB):
                            pe.wait_ge(s_act, a * HB)
                        nc.tensor.matmul(ps_h[:, h, 0:P], w1[:, h * P:(h + 1) * P], source_t[:, bass.ds(a * P, P)],
                                         start=True, stop=True).then_inc(s_h, 1)
                    if later(a):
                        pe.wait_ge(s_ev, a)
                    pe.wait_ge(s_act, (a + 1) * HB)
                    for h in range(HB):
                        mm = nc.tensor.matmul(ps_o[:, 0:D], hidden[:, h, :], w2[:, h, :], start=(h == 0), stop=(h == HB - 1))
                    mm.then_inc(s_o, 1)

            @block.scalar
            def _(act):
                act.wait_ge(s_in, 64)
                @each(act, NT)
                def _(a):
                    if later(a):
                        act.wait_ge(s_o, a)
                    for h in range(HB):
                        act.wait_ge(s_h, a * HB + h + 1)
                        nc.scalar.activation(hidden[:, h, :], ps_h[:, h, 0:P], ACT.Relu, bias=bias[:, h:h + 1]).then_inc(s_act, 1)

            @block.vector
            def _(dve):
                @each(dve, NT)
                def _(a):
                    dve.wait_ge(s_o, a + 1)
                    nc.vector.tensor_copy(target[:, bass.ds(a, 1), :], ps_o[:, 0:D].unsqueeze(1)).then_inc(s_ev, 1)


def normalize(ph, nc, S, dve, ch, y, out):
    mean = ph.sb("mean", [P, NT])
    square = ph.sb("square", [P, NT, D])
    ch.link(nc.vector.tensor_reduce(mean[:], y, AX_X, ALU.add))
    ch.link(nc.vector.tensor_scalar(mean[:], mean[:], 1.0 / D, None, ALU.mult))
    ch.link(nc.vector.tensor_tensor(out, y, wide(mean[:], D), ALU.subtract))
    ch.link(nc.vector.tensor_tensor(square[:], out, out, ALU.mult))
    ch.link(nc.vector.tensor_reduce(S.var[:], square[:], AX_X, ALU.add))
    ready = ch.n
    dve.wait_ge(ph.s_root, 1)
    ch.link(nc.vector.reciprocal(S.var[:], S.var[:]))
    ch.link(nc.vector.tensor_tensor(out, out, wide(S.var[:], D), ALU.mult))
    return ready


def phase_norm(nc, S, name, prepare, out, loads=(), finish=None, bias=None, alpha=None):
    with Phase(nc, name) as ph:
        y = ph.sb("y", [P, NT, D])
        s_dve, s_in = ph.sem("dve"), ph.sem("in")
        ph.s_root, ph.s_alpha = ph.sem("root"), ph.sem("alpha")
        count = {}
        with nc.Block() as block:

            if loads:
                @block.sync
                def _(sp):
                    for target, source in loads:
                        sp.dma_start(target, source).then_inc(s_in, 16)

            @block.vector
            def _(dve):
                ch = Chain(dve, s_dve)
                if loads:
                    dve.wait_ge(s_in, 16 * len(loads))
                count["alpha"] = prepare(dve, ch, y, ph)
                count["var"] = normalize(ph, nc, S, dve, ch, y[:], out[:])
                if finish:
                    finish(ch)

            @block.scalar
            def _(act):
                if alpha is not None:
                    act.wait_ge(s_dve, count["alpha"])
                    nc.scalar.activation(alpha[:], alpha[:], ACT.Sigmoid).then_inc(ph.s_alpha, 1)
                act.wait_ge(s_dve, count["var"])
                nc.scalar.activation(S.var[:], S.var[:], ACT.Sqrt, bias=S.eps[:, 0:1], scale=1.0 / D).then_inc(ph.s_root, 1)


def phase_output(nc, S, source_t, weight, bias, out):
    GROUPS = [range(a, min(a + 4, NT)) for a in range(0, NT, 4)]
    with Phase(nc, "head") as ph:
        w = ph.sb("w", [P, D])
        b = ph.sb("b", [P, D])
        ps = ph.ps("ps", [P, 2, 512])
        s_in, s_mm, s_ev = ph.sem("in"), ph.sem("mm"), ph.sem("ev")
        with nc.Block() as block:

            @block.sync
            def _(sp):
                sp.dma_start(w[:], weight).then_inc(s_in, 16)
                sp.dma_start(b[:], bias.partition_broadcast(P)).then_inc(s_in, 16)

            @block.tensor
            def _(pe):
                pe.wait_ge(s_in, 32)
                for g, tiles in enumerate(GROUPS):
                    if g >= 2:
                        pe.wait_ge(s_ev, g - 1)
                    for c, a in enumerate(tiles):
                        mm = nc.tensor.matmul(ps[:, g % 2, c * P:(c + 1) * P], source_t[:, a * P:(a + 1) * P], w[:], start=True, stop=True)
                    mm.then_inc(s_mm, 1)

            @block.vector
            def _(dve):
                dve.wait_ge(s_in, 32)
                for g, tiles in enumerate(GROUPS):
                    dve.wait_ge(s_mm, g + 1)
                    n = len(tiles)
                    nc.vector.tensor_tensor(S.h[:, g * 4:g * 4 + n, :], ps[:, g % 2, 0:n * P].rearrange("p (a d) -> p a d", d=D),
                                            over(b[:], n), ALU.add).then_inc(s_ev, 1)
    def residual(dve, ch, y, ph):
        ch.link(nc.vector.tensor_tensor(y[:], S.x[:], S.h[:], ALU.add))

    phase_norm(nc, S, "last", residual, S.x)
    with Phase(nc, "store") as ph:
        s_wr = ph.sem("wr")
        with nc.Block() as block:

            @block.sync
            def _(sp):
                full = N_NODES // P
                sp.dma_start(out[0:full * P, :].rearrange("(a p) d -> p a d", p=P), S.x[:, 0:full, :]).then_inc(s_wr, 16)
                sp.dma_start(out[full * P:N_NODES, :], S.x[0:N_NODES - full * P, full, :]).then_inc(s_wr, 16)
                sp.wait_ge(s_wr, 32)


class Arrays:
    pass


def gnn_program(nc, A, out):
    S = Arrays()
    main = ExitStack()

    def sb(scope, name, shape, dt=F32):
        return scope.enter_context(nc.sbuf_tensor(name, shape, dt))

    def dram(name, shape, dt=F32):
        return nc.dram_tensor(name, shape, dt, kind="Internal").ap()

    rec_d_dram, rec_s_dram = dram("rec_d_dram", (NSLOT, RD), I32), dram("rec_s_dram", (NSLOT, RS), I32)
    rows = dram("rows", (N_PAD, D))
    rows8 = dram("rows8", (N_PAD * R8, D))
    k_rows, v_rows = dram("k_rows", (N_PAD * R32, D)), dram("v_rows", (N_PAD * R32, D))

    with main:
        S.iota_row, S.iota_part = sb(main, "iota_row", [P, P]), sb(main, "iota_part", [P, 1])
        S.ident, S.before, S.ones = sb(main, "ident", [P, P]), sb(main, "before", [P, P]), sb(main, "ones", [P, P])
        S.ident4_bf, S.eps = sb(main, "ident4_bf", [P, 4, P], BF16), sb(main, "eps", [P, 1])
        S.sel8, S.sel1 = sb(main, "sel8", [24, HEADS, P], BF16), sb(main, "sel1", [3, P], BF16)
        S.x, S.h = sb(main, "x", [P, NT, D]), sb(main, "h", [P, NT, D])
        S.acc = sb(main, "acc", [P, NT, D + HEADS])
        S.dinv, S.var = sb(main, "dinv", [P, NT]), sb(main, "var", [P, NT])
        S.mx = sb(main, "mx", [P, NT, HEADS])
        rec_d, tile_d = sb(main, "rec_d", [P, NCH, RD], I32), sb(main, "tile_d", [1, NCH], I32)

        phase_constants(nc, S, A["x"], A["node_type"])
        with ExitStack() as first:
            rec_s, tile_s = sb(first, "rec_s", [P, NCH, RS], I32), sb(first, "tile_s", [1, NCH], I32)
            with ExitStack() as edges:
                S.raw, S.weight = sb(edges, "raw", [P, 7, EC], I32), sb(edges, "weight", [P, EC])
                S.src_a, S.src_b, S.dst_a, S.dst_b, S.rel_high, S.score, S.tmp_f = (
                    sb(edges, name, [P, EC]) for name in ("src_a", "src_b", "dst_a", "dst_b", "rel_high", "score", "tmp_f"))
                S.tmp_i, S.row32, S.row8, S.slot = (sb(edges, name, [P, EC], I32) for name in ("tmp_i", "row32", "row8", "slot"))
                phase_edges(nc, S, A)
                phase_rank(nc, S, "rank_s", S.src_a, S.slot, tile_s)
                phase_scatter(nc, S, "scat_s", S.slot,
                              (lambda c: S.raw[:, 3, c], lambda c: S.src_b[:, c].bitcast(I32), lambda c: S.score[:, c].bitcast(I32)),
                              RS, rec_s_dram, rec_s)
                phase_rank(nc, S, "rank_d", S.dst_a, S.slot, tile_d)
                phase_scatter(nc, S, "scat_d", S.slot,
                              (lambda c: S.raw[:, 2, c], lambda c: S.dst_b[:, c].bitcast(I32), lambda c: S.weight[:, c].bitcast(I32),
                               lambda c: S.row8[:, c], lambda c: S.row32[:, c]),
                              RD, rec_d_dram, rec_d)

            S.score_of = sb(first, "score_of0", [P, NCH, 1])
            phase_max(nc, S, "max0", 1, rec_s, tile_s)
            phase_sum(nc, S, "sum0", 1, rec_s, tile_s, A["x"], 0)

        def after_attention(dve, ch, y, ph):
            total = ph.sb("total", [P, NT])
            ch.link(nc.vector.tensor_scalar(total[:], S.acc[:, :, D:D + 1].rearrange("p a o -> p (a o)"), 1e-30, None, ALU.max))
            ch.link(nc.vector.reciprocal(total[:], total[:]))
            ch.link(nc.vector.tensor_tensor(y[:], S.acc[:, :, 0:D], wide(total[:], D), ALU.mult))
            ch.link(nc.vector.scalar_tensor_tensor(out=y[:], in0=y[:], scalar=0.0, in1=S.x[:], op0=ALU.max, op1=ALU.add))
            ch.link(nc.vector.reciprocal(S.dinv[:], S.dinv[:]))

        phase_norm(nc, S, "norm0", after_attention, S.x)

        with ExitStack() as gcn:
            t = sb(gcn, "t", [P, NT, D])
            xt = sb(gcn, "xt1", [P, N_PAD])
            bias = sb(gcn, "b2", [P, D])
            phase_scaled_table(nc, S, "table1", S.x, t, rows)
            phase_sum(nc, S, "sum1", 0, rec_d, tile_d, rows, 0)
            with Phase(nc, "self1") as ph:
                s_dve = ph.sem("dve")
                with nc.Block() as block:

                    @block.vector
                    def _(dve):
                        ch = Chain(dve, s_dve)
                        ch.link(nc.vector.tensor_tensor(t[:], t[:], S.acc[:, :, 0:D], ALU.add))
                        ch.link(nc.vector.tensor_tensor(t[:], t[:], wide(S.dinv[:], D), ALU.mult))

            phase_transpose(nc, S, "tr1", t, xt)
            phase_gcn_dense(nc, S, xt, A["W1"], A["b1"], A["W2"], S.h)
            phase_scaled_table(nc, S, "table2", S.h, t, rows)
            phase_sum(nc, S, "sum2", 0, rec_d, tile_d, rows, 0)

            def after_gcn(dve, ch, y, ph):
                ch.link(nc.vector.tensor_tensor(t[:], t[:], S.acc[:, :, 0:D], ALU.add))
                ch.link(nc.vector.tensor_tensor(t[:], t[:], wide(S.dinv[:], D), ALU.mult))
                ch.link(nc.vector.tensor_tensor(t[:], t[:], over(bias[:], NT), ALU.add))
                ch.link(nc.vector.scalar_tensor_tensor(out=y[:], in0=t[:], scalar=0.0, in1=S.x[:], op0=ALU.max, op1=ALU.add))

            phase_norm(nc, S, "norm1", after_gcn, S.x, loads=((bias[:], A["b2"].partition_broadcast(P)),))

        with ExitStack() as rgcn:
            xt = sb(rgcn, "xt2", [P, N_PAD])
            matrix = sb(rgcn, "matrix2", [P, R8 * D])
            with Phase(nc, "load2") as ph:
                s_in = ph.sem("in")
                with nc.Block() as block:

                    @block.sync
                    def _(sp):
                        sp.dma_start(matrix[:].rearrange("p (t o) -> p t o", t=R8), A["rel_emb"].rearrange("t d o -> d t o")).then_inc(s_in, 16)
                        sp.wait_ge(s_in, 16)

            phase_transpose(nc, S, "tr2", S.x, xt)
            phase_expand(nc, S, "expand2", xt, matrix, rows8)
        phase_sum(nc, S, "sum3", 0, rec_d, tile_d, rows8, 3, weight=True)

        def after_rgcn(dve, ch, y, ph):
            ch.link(nc.vector.tensor_tensor(y[:], S.x[:], S.acc[:, :, 0:D], ALU.add))

        phase_norm(nc, S, "norm2", after_rgcn, S.x)

        for layer in range(LAYERS):
            old = S.x if layer == 0 else S.h
            with ExitStack() as hgt:
                q = sb(hgt, f"q{layer}", [P, NT, D])
                with ExitStack() as pre:
                    kt, vt = sb(pre, f"kt{layer}", [P, N_PAD]), sb(pre, f"vt{layer}", [P, N_PAD])
                    with ExitStack() as tr:
                        xt = sb(tr, f"xt3{layer}", [P, N_PAD])
                        phase_transpose(nc, S, f"tr3{layer}", old, xt)
                        phase_typed(nc, S, f"kqv{layer}", xt, [A["Wk"][layer], A["Wq"][layer], A["Wv"][layer]], A["node_type"],
                                    [(kt, True, ACT.Copy), (q[:].rearrange("p a d -> p (a d)"), False, ACT.Copy), (vt, True, ACT.Copy)])
                    matrix = sb(pre, f"matrix3{layer}", [P, R32 * D])
                    phase_heads(nc, S, f"att{layer}", matrix, A["Watt"][layer], A["pri"][layer])
                    phase_expand(nc, S, f"expk{layer}", kt, matrix, k_rows)
                    phase_heads(nc, S, f"msg{layer}", matrix, A["Wmsg"][layer])
                    phase_expand(nc, S, f"expv{layer}", vt, matrix, v_rows)
                S.score_of = sb(hgt, f"score_of{layer + 1}", [P, NCH, HEADS])
                phase_max(nc, S, f"max{layer + 1}", HEADS, rec_d, tile_d, k_rows, 4, q)
                phase_sum(nc, S, f"sum{layer + 4}", HEADS, rec_d, tile_d, v_rows, 4)
            with ExitStack() as post:
                hag = sb(post, f"hag{layer}", [P, NT, D])
                xt = sb(post, f"xt4{layer}", [P, N_PAD])
                with Phase(nc, f"hag_{layer}") as ph:
                    s_dve = ph.sem("dve")
                    total = ph.sb("total", [P, NT, HEADS])
                    with nc.Block() as block:

                        @block.vector
                        def _(dve):
                            ch = Chain(dve, s_dve)
                            ch.link(nc.vector.tensor_scalar(total[:], S.acc[:, :, D:D + HEADS], 1e-30, None, ALU.max))
                            ch.link(nc.vector.reciprocal(total[:], total[:]))
                            for h in range(HEADS):
                                at = slice(h * HS, (h + 1) * HS)
                                ins = nc.vector.tensor_tensor(hag[:, :, at], S.acc[:, :, at],
                                                              total[:, :, h:h + 1].broadcast_to([P, NT, HS]), ALU.mult)
                            ch.link(ins)

                phase_transpose(nc, S, f"tr4{layer}", hag, xt)
                phase_typed(nc, S, f"wa{layer}", xt, [A["Wa"][layer]], A["node_type"],
                            [(hag[:].rearrange("p a d -> p (a d)"), False, ACT.Silu)])
                alpha = sb(post, f"alpha{layer}", [P, NT])
                type_i = sb(post, f"type_i{layer}", [P, NT], I32)
                skip = sb(post, f"skip{layer}", [P, R16])
                gain, shift = sb(post, f"gain{layer}", [P, D]), sb(post, f"shift{layer}", [P, D])
                hot = sb(post, f"hot{layer}", [P, NT, R16])

                def mix(dve, ch, y, ph):
                    ch.link(nc.vector.tensor_copy(alpha[:], type_i[:]))
                    ch.link(nc.vector.tensor_tensor(hot[:], over(S.iota_row[:, 0:R16], NT), wide(alpha[:], R16), ALU.is_equal))
                    ch.link(nc.vector.tensor_tensor(hot[:], hot[:], over(skip[:], NT), ALU.mult))
                    ch.link(nc.vector.tensor_reduce(alpha[:], hot[:], AX_X, ALU.add))
                    ready = ch.n
                    dve.wait_ge(ph.s_alpha, 1)
                    ch.link(nc.vector.tensor_tensor(y[:], hag[:], old[:], ALU.subtract))
                    ch.link(nc.vector.tensor_tensor(y[:], y[:], wide(alpha[:], D), ALU.mult))
                    ch.link(nc.vector.tensor_tensor(y[:], y[:], old[:], ALU.add))
                    return ready

                def affine(ch):
                    ch.link(nc.vector.tensor_tensor(S.h[:], S.h[:], over(gain[:], NT), ALU.mult))
                    ch.link(nc.vector.tensor_tensor(S.h[:], S.h[:], over(shift[:], NT), ALU.add))

                phase_norm(nc, S, f"norm3{layer}", mix, S.h, finish=affine, alpha=alpha,
                           loads=((type_i[:], A["node_col"]), (skip[:], A["skip"][layer].partition_broadcast(P)),
                                  (gain[:], A["ln_g"][layer].partition_broadcast(P)), (shift[:], A["ln_b"][layer].partition_broadcast(P))))
        with ExitStack() as end:
            xt = sb(end, "xt5", [P, N_PAD])
            phase_transpose(nc, S, "tr5", S.h, xt)
            phase_output(nc, S, xt, A["ff_w"], A["ff_b"], out)


def kernel(**inputs):
    import concourse.bacc as _bacc
    from concourse.bass_utils import run_bass_kernel_spmd as _run

    def column(a, pad):
        flat = np.full(EC * P, pad, a.dtype)
        flat[:N_EDGES] = a
        return np.ascontiguousarray(flat.reshape(EC, P).T)

    def padded(a, n):
        out = np.zeros((n,) + a.shape[1:], a.dtype)
        out[:a.shape[0]] = a
        return out

    g = {k: np.asarray(v) for k, v in inputs.items()}
    types = padded(g["node_type_16"], N_PAD)
    arrays = {
        "x": padded(g["x"], N_PAD), "node_type": types, "node_col": np.ascontiguousarray(types.reshape(NT, P).T),
        "src_key": column(g["src"], N_PAD), "dst_key": column(g["dst"], N_PAD),
        "src_val": column(g["src"], 0), "dst_val": column(g["dst"], 0),
        "rel": column(g["edge_type_1000"], 0), "rel_flat": padded(g["edge_type_1000"], EC * P),
        "type32": column(g["edge_type_32"], 0), "type8": column(g["edge_type_8"], 0), "weight": column(g["edge_weight"], 0),
        "dual_layer": g["L0_gnn_dual_layer"], "conv_w": g["L0_gnn_conv_w"], "conv_b": g["L0_gnn_conv_b"],
        "W1": g["L1_gnn_W1"], "b1": g["L1_gnn_b1"], "W2": g["L1_gnn_W2"], "b2": g["L1_gnn_b2"],
        "rel_emb": g["L2_gnn_rel_emb"],
    }
    for name in ("Wk", "Wq", "Wv", "Wa", "Watt", "Wmsg", "pri", "skip", "ln_g", "ln_b", "ff_w", "ff_b"):
        arrays[name] = g["L3_gnn_" + name]

    nc = _bacc.Bacc("TRN2", target_bir_lowering=False, num_devices=1)
    arrays = {f"in_{n}": np.ascontiguousarray(a) for n, a in arrays.items()}
    A = {n[3:]: nc.dram_tensor(n, a.shape, mybir.dt.from_np(a.dtype), kind="ExternalInput").ap() for n, a in arrays.items()}
    out = nc.dram_tensor("out_0", (N_NODES, D), F32, kind="ExternalOutput").ap()
    gnn_program(nc, A, out)
    r = _run(nc, [arrays], core_ids=[0])
    return r.results[0]["out_0"]
```

```python
from contextlib import ExitStack

import numpy as np

import concourse.bass as bass
from concourse import mybir

F32, BF16, I32, U32 = mybir.dt.float32, mybir.dt.bfloat16, mybir.dt.int32, mybir.dt.uint32
ALU = mybir.AluOpType
ACT = mybir.ActivationFunctionType
AX_X = mybir.AxisListType.X

P = 128
N_NODES, D, N_EDGES = 3125, 128, 103125
NT = -(-N_NODES // P)
N_PAD = NT * P
N_REL, HID = 1000, 256
R8, R16, R32, HEADS, HS, LAYERS = 8, 16, 32, 8, 16, 2
RH = -(-N_REL // P)

EC = -(-N_EDGES // P)
EG = 13
EI = EC // (2 * EG)
assert EC == 2 * EG * EI

GC = 8
NCH = -(-((N_EDGES + NT * (P - 1)) // P + 1) // (2 * GC)) * 2 * GC
IT = NCH // (2 * GC)
NSLOT = NCH * P
RD, RS = 5, 3
BIG = float(2.0 ** 100)
EPS = 1e-5


class Phase:

    def __init__(self, nc, name):
        self.nc, self.name, self.ctx, self.sems = nc, name, ExitStack(), []

    def sb(self, name, shape, dt=F32):
        return self.ctx.enter_context(self.nc.sbuf_tensor(f"{self.name}_{name}", shape, dt))

    def ps(self, name, shape, dt=F32):
        return self.ctx.enter_context(self.nc.psum_tensor(f"{self.name}_{name}", shape, dt))

    def sem(self, name):
        s = self.nc.alloc_semaphore(f"{self.name}_{name}")
        self.sems.append(s)
        return s

    def __enter__(self):
        return self

    def __exit__(self, *exc):
        if exc[0] is None:
            self.nc.clear_and_free_semaphores(self.sems)
            self.nc.all_engine_barrier()
        self.ctx.close()
        return False


class Chain:

    def __init__(self, eng, sem):
        self.eng, self.sem, self.n = eng, sem, 0

    def link(self, ins):
        self.n += 1
        ins.then_inc(self.sem, 1)
        self.eng.wait_ge(self.sem, self.n)


def each(eng, n):
    def run(body):
        body(0)
        with eng.Fori(1, n) as i:
            body(i)
    return run


def both_ends(eng, n):
    def run(body):
        body(0, True, False)
        with eng.Fori(1, n - 1) as i:
            body(i, False, False)
        body(n - 1, False, True)
    return run


def later(count):
    return not (isinstance(count, int) and count == 0)


def load_tiles(nc, eng_type, tile_of, g, n):
    _, tiles = nc.values_load_multi_w_load_instructions(
        tile_of[0:1, bass.ds(g * GC, n)], engines=[eng_type], min_val=0, max_val=NT - 1,
        skip_runtime_bounds_check_because="a count of tiles that start at the chunk or before, less one")
    return list(tiles)


def wide(ap, n):
    return ap.unsqueeze(2).broadcast_to([ap.shape[0], ap.shape[1], n])


def over(ap, n):
    return ap.unsqueeze(1).broadcast_to([ap.shape[0], n, ap.shape[1]])


def phase_constants(nc, S, x):
    with Phase(nc, "const") as ph:
        s_iota, s_ident, s_load, s_dve = (ph.sem(n) for n in ("iota", "ident", "load", "dve"))
        with nc.Block() as block:

            @block.gpsimd
            def _(pool):
                nc.gpsimd.iota(S.chunk_no[:], [[1, NCH]], base=0, channel_multiplier=0,
                               allow_small_or_imprecise_dtypes=True)
                nc.gpsimd.iota(S.iota_row[:], [[1, P]], base=0, channel_multiplier=0,
                               allow_small_or_imprecise_dtypes=True).then_inc(s_iota, 1)
                nc.gpsimd.iota(S.iota_part[:], [[1, 1]], base=0, channel_multiplier=1,
                               allow_small_or_imprecise_dtypes=True).then_inc(s_iota, 1)

            @block.sync
            def _(sp):
                sp.dma_start(S.x[:], x.rearrange("(a p) d -> p a d", p=P)).then_inc(s_load, 16)
                sp.wait_ge(s_load, 16)

            @block.vector
            def _(dve):
                ch = Chain(dve, s_dve)
                dve.wait_ge(s_iota, 2)
                nc.vector.tensor_scalar(S.ident[:], S.iota_row[:], S.iota_part[:, 0:1], None, ALU.is_equal)
                nc.vector.tensor_scalar(S.before[:], S.iota_row[:], S.iota_part[:, 0:1], None, ALU.is_gt)
                nc.vector.memset(S.ones[:], 1.0)
                for j in range(4):
                    nc.vector.tensor_scalar(S.ident4_bf[:, j, :], S.iota_row[:], S.iota_part[:, 0:1], None,
                                            ALU.is_equal)
                nc.vector.memset(S.eps[:], EPS).then_inc(s_ident, 1)
                ch.link(nc.vector.memset(S.sel1[:], 1.0))


def phase_edges(nc, S, T, empty):
    W = EG * P
    with Phase(nc, "edge") as ph:
        dual = ph.sb("dual", [P, RH, 2 * D])
        conv_w = ph.sb("conv_w", [P, 2 * D])
        conv_b = ph.sb("conv_b", [P, 1])
        logit = ph.sb("logit", [P, RH])
        scaled = ph.sb("scaled", [P, RH])
        table = ph.sb("table", [P, RH])
        rel_row = ph.sb("rel_row", [P, 2, W], I32)
        low_row = ph.sb("low_row", [P, 2, W], I32)
        hot_low = ph.sb("hot_low", [P, 2, W])
        hot_high = ph.sb("hot_high", [P, EG, RH])
        picked = ph.sb("picked", [P, EG, RH])
        hot_b = ph.sb("hot_b", [P, 2, EG, P], BF16)
        hot_a = ph.sb("hot_a", [P, 2, EG, NT], BF16)
        zeros = ph.sb("zeros", [P, P], BF16)
        ps_rel = ph.ps("rel", [P, 2, 512])
        ps_deg = ph.ps("deg", [P, 512])
        s_in, s_dve, s_zero, s_deg = (ph.sem(n) for n in ("in", "dve", "zero", "deg"))
        s_row = [ph.sem(f"row{k}") for k in range(2)]
        s_low = [ph.sem(f"low{k}") for k in range(2)]
        s_hot = [ph.sem(f"hot{k}") for k in range(2)]
        s_rel = [ph.sem(f"rel{k}") for k in range(2)]
        s_hots = [ph.sem(f"hots{k}") for k in range(2)]
        s_cnt = [ph.sem(f"cnt{k}") for k in range(2)]
        s_out = [ph.sem(f"out{k}") for k in range(2)]
        s_pick, s_fill, s_wr = (ph.sem(n) for n in ("pick", "fill", "wr"))
        with nc.Block() as block:

            @block.sync
            def _(sp):
                full = (RH - 1) * P
                sp.dma_start(dual[:, 0:RH - 1, :], T["dual_layer"][0:full, :].rearrange("(h p) d -> p h d", p=P)).then_inc(s_in, 16)
                sp.wait_ge(s_zero, 1)
                sp.dma_start(dual[0:N_REL - full, RH - 1, :], T["dual_layer"][full:N_REL, :]).then_inc(s_in, 16)
                sp.dma_start(conv_w[:], T["conv_w"].rearrange("d o -> (o d)").partition_broadcast(P)).then_inc(s_in, 16)
                sp.dma_start(conv_b[:], T["conv_b"].partition_broadcast(P)).then_inc(s_in, 16)
                for k, name in enumerate(("src_key", "dst_key", "src_val", "dst_val", "rel", "type32", "type8")):
                    sp.dma_start(S.raw[:, k, :], T[name]).then_inc(s_in, 16)
                sp.dma_start(S.weight[:], T["weight"]).then_inc(s_in, 16)
                @each(sp, EI)
                def _(i):
                    for k in range(2):
                        if later(i):
                            sp.wait_ge(s_low[k], i)
                        sp.dma_start(rel_row[:, k, :], T["rel_flat"][bass.ds((i * 2 + k) * W, W)].partition_broadcast(P)).then_inc(s_row[k], 16)
                for n, (kept, records) in enumerate(empty):
                    sp.wait_ge(s_fill, 2 * (n + 1))
                    sp.dma_start(records.rearrange("(p c) w -> p (c w)", p=P), kept[:].rearrange("p c w -> p (c w)")).then_inc(s_wr, 16)
                sp.wait_ge(s_wr, 16 * len(empty))

            @block.vector
            def _(dve):
                ch = Chain(dve, s_dve)
                nc.vector.memset(zeros[:], 0.0)
                nc.vector.memset(dual[:, RH - 1, :], 0.0).then_inc(s_zero, 1)
                for n, (kept, _) in enumerate(empty):
                    nc.vector.memset(kept[:], 0).then_inc(s_fill, 1)
                    dve.wait_ge(s_fill, 2 * n + 1)
                    nc.vector.memset(kept[:, :, 1:2].bitcast(F32), -1.0).then_inc(s_fill, 1)
                dve.wait_ge(s_in, 12 * 16)
                ch.link(nc.vector.tensor_tensor(dual[:], dual[:], over(conv_w[:], RH), ALU.mult))
                ch.link(nc.vector.tensor_reduce(logit[:], dual[:], AX_X, ALU.add))
                ch.link(nc.vector.tensor_scalar(logit[:], logit[:], conv_b[:, 0:1], None, ALU.add))
                ch.link(nc.vector.tensor_scalar(scaled[:], logit[:], 0.01, None, ALU.mult))
                ch.link(nc.vector.tensor_tensor(table[:], logit[:], scaled[:], ALU.max))
                for key, tile, row in ((0, S.src_a, S.src_b), (1, S.dst_a, S.dst_b)):
                    ch.link(nc.vector.tensor_scalar(S.tmp_i[:], S.raw[:, key, :], 7, None, ALU.logical_shift_right))
                    ch.link(nc.vector.tensor_copy(tile[:], S.tmp_i[:]))
                    ch.link(nc.vector.tensor_scalar(S.tmp_i[:], S.raw[:, key, :], P - 1, None, ALU.bitwise_and))
                    ch.link(nc.vector.tensor_scalar(S.tmp_f[:], tile[:], float(NT), -1000.0, ALU.is_ge, ALU.mult))
                    ch.link(nc.vector.tensor_tensor(row[:], S.tmp_f[:], S.tmp_i[:], ALU.add))
                ch.link(nc.vector.tensor_scalar(S.tmp_i[:], S.raw[:, 4, :], 7, None, ALU.logical_shift_right))
                ch.link(nc.vector.tensor_copy(S.rel_high[:], S.tmp_i[:]))
                ch.link(nc.vector.scalar_tensor_tensor(out=S.row32[:], in0=S.raw[:, 2, :], scalar=float(R32),
                                                       in1=S.raw[:, 5, :], op0=ALU.mult, op1=ALU.add))
                ch.link(nc.vector.scalar_tensor_tensor(out=S.row8[:], in0=S.raw[:, 2, :], scalar=float(R8),
                                                       in1=S.raw[:, 6, :], op0=ALU.mult, op1=ALU.add))
                def low_one_hot(k, n):
                    dve.wait_ge(s_row[k], (n + 1) * 16)
                    nc.vector.tensor_scalar(low_row[:, k, :], rel_row[:, k, :], P - 1, None, ALU.bitwise_and).then_inc(s_low[k], 1)
                    dve.wait_ge(s_low[k], n + 1)
                    if later(n):
                        dve.wait_ge(s_rel[k], n)
                    nc.vector.tensor_scalar(hot_low[:, k, :], low_row[:, k, :], S.iota_part[:, 0:1], None,
                                            ALU.is_equal).then_inc(s_hot[k], 1)

                low_one_hot(0, 0)

                @both_ends(dve, EI)
                def _(i, first, last):
                    for k in range(2):
                        cols = bass.ds((i * 2 + k) * EG, EG)
                        if not (last and k):
                            low_one_hot(1 - k, i + k)
                        if later(i):
                            dve.wait_ge(s_cnt[k], i)
                        nc.vector.tensor_tensor(hot_b[:, k], over(S.iota_row[:], EG), wide(S.dst_b[:, cols], P), ALU.is_equal)
                        nc.vector.tensor_tensor(hot_a[:, k], over(S.iota_row[:, 0:NT], EG), wide(S.dst_a[:, cols], NT),
                                                ALU.is_equal).then_inc(s_hots[k], 1)
                        nc.vector.tensor_tensor(hot_high[:], over(S.iota_row[:, 0:RH], EG), wide(S.rel_high[:, cols], RH),
                                                ALU.is_equal).then_inc(s_pick, 1)
                        dve.wait_ge(s_pick, i * 4 + 2 * k + 1)
                        dve.wait_ge(s_rel[k], i + 1)
                        nc.vector.tensor_tensor(picked[:], ps_rel[:, k, 0:EG * RH].rearrange("p (c h) -> p c h", h=RH),
                                                hot_high[:], ALU.mult).then_inc(s_pick, 1)
                        dve.wait_ge(s_pick, i * 4 + 2 * k + 2)
                        nc.vector.tensor_reduce(S.score[:, cols], picked[:], AX_X, ALU.add).then_inc(s_out[k], 1)
                dve.wait_ge(s_out[1], EI)
                dve.wait_ge(s_deg, 1)
                ch.link(nc.vector.tensor_scalar(S.dinv[:], ps_deg[:, 0:NT], 1.0, None, ALU.add))

            @block.scalar
            def _(act):
                act.wait_ge(s_dve, 20)
                nc.scalar.activation(S.dinv[:], S.dinv[:], ACT.Sqrt).then_inc(s_zero, 1)

            @block.tensor
            def _(pe):
                pe.wait_ge(s_zero, 1)
                nc.tensor.matmul(ps_deg[:, 0:NT], zeros[:], zeros[:, 0:NT], start=True, stop=False, skip_group_check=True)
                @each(pe, EI)
                def _(i):
                    for k in range(2):
                        pe.wait_ge(s_hot[k], i + 1)
                        if later(i):
                            pe.wait_ge(s_out[k], i)
                        for c in range(EG):
                            mm = nc.tensor.matmul(ps_rel[:, k, c * RH:(c + 1) * RH], hot_low[:, k, c * P:(c + 1) * P], table[:],
                                                  start=True, stop=True)
                        mm.then_inc(s_rel[k], 1)
                        pe.wait_ge(s_hots[k], i + 1)
                        for c in range(EG):
                            mm = nc.tensor.matmul(ps_deg[:, 0:NT], hot_b[:, k, c, :], hot_a[:, k, c, :],
                                                  start=False, stop=False, skip_group_check=True)
                        mm.then_inc(s_cnt[k], 1)
                nc.tensor.matmul(ps_deg[:, 0:NT], zeros[:], zeros[:, 0:NT], start=False, stop=True, skip_group_check=True).then_inc(s_deg, 1)


def rank_program(nc, S, tile, slot, tile_of, packed, fields):
    NB = NT + 1

    def program(ph, block):
        mask = ph.sb("mask", [P, EC])
        zeros = ph.sb("zeros", [P, EC])
        rank = ph.sb("rank", [P, EC])
        place = ph.sb("place", [P, EC])
        count = ph.sb("count", [P, NB])
        chunks_i = ph.sb("chunks_i", [P, NB], I32)
        chunks = ph.sb("chunks", [P, NB])
        last = ph.sb("last", [P, NB])
        start = ph.sb("start", [P, NB])
        tiles_i = ph.sb("tiles_i", [NT, 1], I32)
        tiles = ph.sb("tiles", [NT, 1])
        first = ph.sb("first", [NT, 1])
        past = ph.sb("past", [NT, NCH])
        ps = ph.ps("ps", [P, 512])
        ps_t = ph.ps("ps_t", [P, 512])
        ps_c = ph.ps("ps_c", [1, 2, 512])
        s_dve, s_pe, s_it = (ph.sem(n) for n in ("dve", "pe", "it"))

        @block.vector
        def _(dve):
            ch = Chain(dve, s_dve)
            nc.vector.memset(zeros[:], 0.0)
            for f, (dt, columns) in enumerate(fields):
                word = packed[:, :, f]
                nc.vector.tensor_copy(word if dt == I32 else word.bitcast(dt), columns)
            ch.link(nc.vector.memset(place[:], 0.0))
            @each(dve, NB)
            def _(t):
                if later(t):
                    dve.wait_ge(s_it, t)
                nc.vector.tensor_scalar(mask[:], tile[:], S.iota_row[:, bass.ds(t, 1)], 0.0, ALU.is_equal, ALU.add,
                                        accum_out=count[:, bass.ds(t, 1)]).then_inc(s_it, 1)
            dve.wait_ge(s_pe, 1)
            for n_i, n, tot in ((chunks_i, chunks, ps[:, 64:64 + NB]), (tiles_i, tiles, ps_t[0:NT, 0:1])):
                ch.link(nc.vector.tensor_scalar(n_i[:], tot, float(P - 1), None, ALU.add))
                ch.link(nc.vector.tensor_scalar(n_i[:], n_i[:], 7, None, ALU.logical_shift_right))
                ch.link(nc.vector.tensor_copy(n[:], n_i[:]))
            ch.link(nc.vector.tensor_tensor_scan(last[:], chunks[:], zeros[:, 0:NB], 0.0, ALU.add, ALU.add))
            ch.link(nc.vector.tensor_tensor(start[:], last[:], chunks[:], ALU.subtract))
            ch.link(nc.vector.tensor_scalar(start[:], start[:], float(P), -1.0, ALU.mult, ALU.add))
            ch.link(nc.vector.tensor_tensor(start[:], start[:], ps[:, 0:NB], ALU.add))
            @each(dve, NB)
            def _(t):
                if later(t * 4 + NB):
                    dve.wait_ge(s_it, t * 4 + NB)
                nc.vector.tensor_scalar(mask[:], tile[:], S.iota_row[:, bass.ds(t, 1)], None, ALU.is_equal).then_inc(s_it, 1)
                dve.wait_ge(s_it, t * 4 + NB + 1)
                nc.vector.tensor_tensor_scan(rank[:], mask[:], zeros[:], start[:, bass.ds(t, 1)], ALU.add, ALU.add).then_inc(s_it, 1)
                dve.wait_ge(s_it, t * 4 + NB + 2)
                nc.vector.tensor_tensor(rank[:], rank[:], mask[:], ALU.mult).then_inc(s_it, 1)
                dve.wait_ge(s_it, t * 4 + NB + 3)
                nc.vector.tensor_tensor(place[:], place[:], rank[:], ALU.add).then_inc(s_it, 1)
            dve.wait_ge(s_it, NB * 5)
            ch.link(nc.vector.tensor_copy(slot[:], place[:]))
            ch.link(nc.vector.tensor_scalar(S.tmp_i[:], slot[:], 7, None, ALU.logical_shift_right))
            ch.link(nc.vector.tensor_scalar(slot[:], slot[:], P - 1, None, ALU.bitwise_and))
            ch.link(nc.vector.scalar_tensor_tensor(out=slot[:], in0=slot[:], scalar=float(NCH), in1=S.tmp_i[:],
                                                   op0=ALU.mult, op1=ALU.add))
            dve.wait_ge(s_pe, 2)
            ch.link(nc.vector.tensor_copy(first[:], ps_t[0:NT, 1:2]))
            ch.link(nc.vector.tensor_scalar(past[:], S.chunk_no[:], first[:, 0:1], None, ALU.is_ge))
            dve.wait_ge(s_pe, 3)
            ch.link(nc.vector.tensor_scalar(tile_of[:].rearrange("p (h c) -> p h c", h=2),
                                            ps_c[0:1, :, 0:NCH // 2], -1.0, None, ALU.add))

        @block.tensor
        def _(pe):
            pe.wait_ge(s_it, NB)
            nc.tensor.matmul(ps[:, 0:NB], S.before[:], count[:], start=True, stop=True)
            nc.tensor.matmul(ps[:, 64:64 + NB], S.ones[:], count[:], start=True, stop=True)
            nc.tensor.matmul(ps_t[0:NT, 0:1], count[:, 0:NT], S.ones[:, 0:1], start=True, stop=True).then_inc(s_pe, 1)
            pe.wait_ge(s_dve, 7)
            nc.tensor.matmul(ps_t[0:NT, 1:2], S.before[0:NT, 0:NT], tiles[:], start=True, stop=True).then_inc(s_pe, 1)
            pe.wait_ge(s_dve, 17)
            for h in range(2):
                mm = nc.tensor.matmul(ps_c[0:1, h, 0:NCH // 2], S.ones[0:NT, 0:1], past[:, h * NCH // 2:(h + 1) * NCH // 2],
                                      start=True, stop=True)
            mm.then_inc(s_pe, 1)

    return program


def phase_rank(nc, S, name, program):
    with Phase(nc, name) as ph:
        with nc.Block() as block:
            program(ph, block)


def phase_scatter(nc, S, name, slot, packed, words, records, kept, beside=None):
    with Phase(nc, name) as ph:
        stage = ph.sb("stage", [P, 2, EG, words], I32)
        slots = ph.sb("slots", [P, 2, EG], I32)
        s_load, s_go = ph.sem("load"), ph.sem("go")
        s_stage = [ph.sem(f"stage{k}") for k in range(2)]
        s_scat = [ph.sem(f"scat{k}") for k in range(2)]
        with nc.Block() as block:

            @block.gpsimd
            def _(pool):
                @each(pool, EI)
                def _(i):
                    for k in range(2):
                        pool.wait_ge(s_stage[k], (i + 1) * 32)
                        pool.sem_inc(s_go, 1)
                        for c in range(EG):
                            pool.indirect_dma_start(records, bass.IndirectOffsetOnAxis(ap=slots[:, k, c:c + 1].bitcast(U32), axis=0),
                                                    stage[:, k, c, :], None).then_inc(s_scat[k], 16)

            @block.sync
            def _(sp):
                @each(sp, EI)
                def _(i):
                    for k in range(2):
                        cols = bass.ds((i * 2 + k) * EG, EG)
                        if later(i):
                            sp.wait_ge(s_scat[k], i * (EG * 16))
                        sp.dma_start(stage[:, k], packed[:, cols, :]).then_inc(s_stage[k], 16)
                        sp.dma_start(slots[:, k, :], slot[:, cols]).then_inc(s_stage[k], 16)
                sp.wait_ge(s_scat[0], EI * EG * 16)
                sp.wait_ge(s_scat[1], EI * EG * 16)
                sp.dma_start(kept[:].rearrange("p c w -> p (c w)"), records.rearrange("(p c) w -> p (c w)", p=P)).then_inc(s_load, 16)
                sp.wait_ge(s_load, 16)

            if beside:
                beside(ph, block)


def max_program(nc, S, records, tile_of):
    def program(ph, block):
        hot = ph.sb("hot", [P, 2, GC, P], BF16)
        miss = ph.sb("miss", [P, 2, GC, P], BF16)
        part = ph.sb("part", [P, NCH, 3], BF16)
        rest = ph.sb("rest", [P, NCH, 1])
        parts_t = ph.sb("parts_t", [3, 2, GC * P], BF16)
        top = ph.sb("top", [P, 2, GC])
        ps_m = ph.ps("m", [P, 2, 1024])
        ps_p = ph.ps("p", [3, 2, GC * P])
        s_hot, s_miss, s_pt, s_cp, s_full, s_read = ([ph.sem(f"{n}{k}") for k in range(2)]
                                                     for n in ("hot", "miss", "pt", "cp", "full", "read"))
        s_split, s_up = ph.sem("split"), ph.sem("up")
        fields = records[:].bitcast(F32)

        @block.vector
        def _(dve):
            def one_hot(g, k, n):
                if later(n):
                    dve.wait_ge(s_miss[k], n)
                nc.vector.tensor_tensor(hot[:, k], over(S.iota_row[:], GC), wide(fields[:, bass.ds(g * GC, GC), 1], P),
                                        ALU.is_equal).then_inc(s_hot[k], 1)

            ch = Chain(dve, s_split)
            nc.vector.memset(S.mx[:], -BIG)
            ch.link(nc.vector.tensor_copy(S.score_of[:], fields[:, :, 2:3]))
            ch.link(nc.vector.tensor_copy(part[:, :, 0:1], S.score_of[:]))
            ch.link(nc.vector.tensor_tensor(rest[:], S.score_of[:], part[:, :, 0:1], ALU.subtract))
            ch.link(nc.vector.tensor_copy(part[:, :, 1:2], rest[:]))
            ch.link(nc.vector.tensor_tensor(rest[:], rest[:], part[:, :, 1:2], ALU.subtract))
            ch.link(nc.vector.tensor_copy(part[:, :, 2:3], rest[:]))
            one_hot(0, 0, 0)

            @both_ends(dve, IT)
            def _(i, first, last):
                tiles = load_tiles(nc, mybir.EngineType.DVE, tile_of, i * 2, 2 * GC)
                for k in range(2):
                    g = i * 2 + k
                    if not (last and k):
                        one_hot(g + 1, 1 - k, i + k)
                    dve.wait_ge(s_full[k], i + 1)
                    nc.vector.tensor_reduce(top[:, k], ps_m[:, k, :].rearrange("p (c e) -> p c e", e=P), AX_X,
                                            ALU.max).then_inc(s_read[k], 1)
                    dve.wait_ge(s_read[k], i + 1)
                    for c in range(GC):
                        mx = S.mx[:, bass.ds(tiles[k * GC + c], 1), 0]
                        nc.vector.tensor_tensor(mx, mx, top[:, k, c:c + 1], ALU.max).then_inc(s_up, 1)
                        dve.wait_ge(s_up, g * GC + c + 1)

        @block.scalar
        def _(act):
            @each(act, IT)
            def _(i):
                for k in range(2):
                    act.wait_ge(s_hot[k], i + 1)
                    if later(i):
                        act.wait_ge(s_full[k], i)
                    nc.scalar.activation(miss[:, k], hot[:, k], ACT.Copy, bias=-BIG, scale=BIG).then_inc(s_miss[k], 1)
                    act.wait_ge(s_pt[k], i + 1)
                    nc.scalar.copy(parts_t[:, k, :], ps_p[:, k, :]).then_inc(s_cp[k], 1)

        @block.tensor
        def _(pe):
            def turn(g, k, n):
                if later(n):
                    pe.wait_ge(s_cp[k], n)
                for c in range(GC):
                    mm = nc.tensor.matmul(ps_p[:, k, c * P:(c + 1) * P],
                                          part[:, bass.ds(g * GC + c, 1), :].rearrange("p a w -> p (a w)"), S.ident4_bf[:, 0, :],
                                          start=True, stop=True)
                mm.then_inc(s_pt[k], 1)

            pe.wait_ge(s_split, 6)
            turn(0, 0, 0)

            @both_ends(pe, IT)
            def _(i, first, last):
                for k in range(2):
                    g = i * 2 + k
                    if not (last and k):
                        turn(g + 1, 1 - k, i + k)
                    pe.wait_ge(s_cp[k], i + 1)
                    pe.wait_ge(s_miss[k], i + 1)
                    if later(i):
                        pe.wait_ge(s_read[k], i)
                    for b in range(2):
                        bank = ps_m[:, k, b * 512:(b + 1) * 512]
                        nc.tensor.matmul(bank, S.sel1[:], parts_t[:, k, b * 512:(b + 1) * 512], start=True, stop=False,
                                         skip_group_check=True)
                        for c in range(4):
                            mm = nc.tensor.matmul(bank[:, c * P:(c + 1) * P], miss[:, k, b * 4 + c, :], S.ident4_bf[:, 0, :],
                                                  start=False, stop=(c == 3), skip_group_check=True)
                    mm.then_inc(s_full[k], 1)

    return program


def phase_order(nc, S, rec, key_of):
    BLOCKS = [(b, min(P, NCH - b * P)) for b in range(-(-NCH // P))]
    fields = rec[:].bitcast(F32)
    with Phase(nc, "order") as ph:
        key = ph.sb("key", [P, NCH])
        key_t = ph.sb("key_t", [P, len(BLOCKS), P])
        key_row = ph.sb("key_row", [P, 2, GC * P])
        below = ph.sb("below", [P, 2, GC, P], BF16)
        ones = ph.sb("ones", [P, 1], BF16)
        rank = ph.sb("rank", [P, 2, GC])
        move = ph.sb("move", [P, 2, GC, P])
        values = ph.sb("values", [P, 2, GC, RD])
        ps_k = ph.ps("k", [P, 2, 4, P])
        ps_r = [ph.ps(f"r{k}", [P, 512]) for k in range(2)]
        ps_f = [ph.ps(f"f{k}", [P, 512]) for k in range(2)]
        s_key, s_tr, s_cp, s_wr = (ph.sem(n) for n in ("key", "tr", "cp", "wr"))
        s_row, s_below, s_count, s_rank, s_move, s_moved, s_back = (
            [ph.sem(f"{n}{k}") for k in range(2)] for n in ("row", "below", "count", "rank", "move", "moved", "back"))
        with nc.Block() as block:

            @block.sync
            def _(sp):
                for b, n in BLOCKS:
                    sp.wait_ge(s_cp, b + 1)
                    sp.dma_start(key_of[b * P * P:(b * P + n) * P].rearrange("(n e) -> n e", e=P), key_t[0:n, b, :]).then_inc(s_wr, 16)
                sp.wait_ge(s_wr, len(BLOCKS) * 16)
                @each(sp, IT)
                def _(i):
                    for k in range(2):
                        if later(i):
                            sp.wait_ge(s_below[k], i)
                        sp.dma_start(key_row[:, k, :], key_of[bass.ds((i * 2 + k) * (GC * P), GC * P)].partition_broadcast(P)).then_inc(s_row[k], 16)

            @block.scalar
            def _(act):
                act.wait_ge(s_tr, 1)
                for b, n in BLOCKS:
                    nc.scalar.copy(key_t[0:n, b, :], ps_k[0:n, b // 4, b % 4, :]).then_inc(s_cp, 1)
                @each(act, IT)
                def _(i):
                    for k in range(2):
                        act.wait_ge(s_moved[k], i + 1)
                        moved = ps_f[k][:, 0:GC * RD].rearrange("p (c w) -> p c w", w=RD)
                        cols = bass.ds((i * 2 + k) * GC, GC)
                        nc.scalar.copy(rec[:, cols, 0:1], moved[:, :, 0:1])
                        nc.scalar.copy(fields[:, cols, 1:3], moved[:, :, 1:3])
                        nc.scalar.copy(rec[:, cols, 3:RD], moved[:, :, 3:RD]).then_inc(s_back[k], 1)

            @block.vector
            def _(dve):
                def compare(g, k, n):
                    dve.wait_ge(s_row[k], (n + 1) * 16)
                    if later(n):
                        dve.wait_ge(s_count[k], n)
                    nc.vector.tensor_tensor(below[:, k], key_row[:, k, :].rearrange("p (c e) -> p c e", e=P),
                                            wide(key[:, bass.ds(g * GC, GC)], P), ALU.is_gt).then_inc(s_below[k], 1)

                nc.vector.memset(ones[:], 1.0)
                nc.vector.tensor_scalar(key[:], fields[:, :, 1:2].rearrange("p c o -> p (c o)"), float(P), S.iota_part[:, 0:1],
                                        ALU.mult, ALU.add).then_inc(s_key, 1)
                dve.wait_ge(s_key, 1)
                compare(0, 0, 0)
                compare(1, 1, 0)

                @both_ends(dve, IT)
                def _(i, first, last):
                    for k in range(2):
                        g = i * 2 + k
                        cols = bass.ds(g * GC, GC)
                        if later(i):
                            dve.wait_ge(s_moved[k], i)
                        nc.vector.tensor_scalar(values[:, k, :, 0:1], rec[:, cols, 0:1], 1.0, None, ALU.mult)
                        nc.vector.tensor_copy(values[:, k, :, 1:3], fields[:, cols, 1:3])
                        nc.vector.tensor_copy(values[:, k, :, 3:RD], rec[:, cols, 3:RD])
                        dve.wait_ge(s_count[k], i + 1)
                        nc.vector.tensor_scalar(rank[:, k], ps_r[k][:, 0:GC], 1.0, None, ALU.mult).then_inc(s_rank[k], 1)
                        dve.wait_ge(s_rank[k], i + 1)
                        nc.vector.tensor_tensor(move[:, k], over(S.iota_row[:], GC), wide(rank[:, k], P), ALU.is_equal).then_inc(s_move[k], 1)
                        if not last:
                            compare(g + 2, k, i + 1)

            @block.tensor
            def _(pe):
                def ranks(k, n):
                    pe.wait_ge(s_below[k], n + 1)
                    if later(n):
                        pe.wait_ge(s_rank[k], n)
                    for c in range(GC):
                        mm = nc.tensor.matmul(ps_r[k][:, c:c + 1], below[:, k, c, :], ones[:], start=True, stop=True)
                    mm.then_inc(s_count[k], 1)

                pe.wait_ge(s_key, 1)
                for b, n in BLOCKS:
                    mm = nc.tensor.transpose(ps_k[0:n, b // 4, b % 4, :], key[:, b * P:b * P + n], S.ident[:])
                mm.then_inc(s_tr, 1)
                ranks(0, 0)

                @both_ends(pe, IT)
                def _(i, first, last):
                    for k in range(2):
                        if not (last and k):
                            ranks(1 - k, i + k)
                        pe.wait_ge(s_move[k], i + 1)
                        if later(i):
                            pe.wait_ge(s_back[k], i)
                        for c in range(GC):
                            mm = nc.tensor.matmul(ps_f[k][:, c * RD:(c + 1) * RD], move[:, k, c, :], values[:, k, c, :],
                                                  start=True, stop=True)
                        mm.then_inc(s_moved[k], 1)


def phase_segments(nc, S, rec):
    fields = rec[:].bitcast(F32)
    BLOCKS = [(b, min(P, NCH - b * P)) for b in range(-(-NCH // P))]
    NB, GB = len(BLOCKS), P // GC
    NG = NCH // GC
    with Phase(nc, "segments") as ph:
        row = ph.sb("row", [P, NB, P])
        ends = ph.sb("ends", [P, NB, P])
        starts = ph.sb("starts", [P, NB, P], BF16)
        gap = ph.sb("gap", [P, GB, GC, HEADS])
        pick = ph.sb("pick", [P, GB, GC * HEADS], BF16)
        ps_a = ph.ps("a", [P, 2, 4, P])
        ps_p = ph.ps("p", [GC * HEADS, 2, 512])
        s_iota, s_dve, s_tr, s_cp, s_pick, s_out, s_end = (ph.sem(n) for n in ("iota", "dve", "tr", "cp", "pick", "out", "end"))
        with nc.Block() as block:

            @block.gpsimd
            def _(pool):
                nc.gpsimd.iota(gap[:], [[-GC, GB], [-1, GC], [0, HEADS]], base=0, channel_multiplier=1,
                               allow_small_or_imprecise_dtypes=True).then_inc(s_iota, 1)

            @block.tensor
            def _(pe):
                for b, n in BLOCKS:
                    mm = nc.tensor.transpose(ps_a[0:n, b // 4, b % 4, :], fields[:, b * P:b * P + n, 1:2].rearrange("p c o -> p (c o)"),
                                             S.ident[:])
                mm.then_inc(s_tr, 1)
                pe.wait_ge(s_dve, 6)
                for b, n in BLOCKS:
                    mm = nc.tensor.transpose(ps_a[:, b // 4, b % 4, 0:n], ends[0:n, b, :], S.ident[0:n, 0:n])
                mm.then_inc(s_end, 1)
                for g in range(NG):
                    b, n = BLOCKS[g // GB]
                    if g % 4 == 0 and g >= 8:
                        pe.wait_ge(s_out, g // 4 - 1)
                    mm = nc.tensor.matmul(ps_p[:, g // 4 % 2, (g % 4) * P:(g % 4 + 1) * P], pick[0:n, g % GB, :], starts[0:n, b, :],
                                          start=True, stop=True)
                    if g % 4 == 3:
                        mm.then_inc(s_pick, 1)

            @block.scalar
            def _(act):
                act.wait_ge(s_dve, 1)
                act.wait_ge(s_tr, 1)
                for b, n in BLOCKS:
                    cp = nc.scalar.copy(row[0:n, b, :], ps_a[0:n, b // 4, b % 4, :])
                cp.then_inc(s_cp, 1)
                act.wait_ge(s_end, 1)
                for b, n in BLOCKS:
                    nc.scalar.copy(S.last[:, b * P:b * P + n], ps_a[:, b // 4, b % 4, 0:n])
                for m in range(NG // 4):
                    act.wait_ge(s_pick, m + 1)
                    nc.scalar.copy(S.reset[:, m * 4:m * 4 + 4, :].rearrange("p g e -> p (g e)"), ps_p[:, m % 2, :]).then_inc(s_out, 1)

            @block.vector
            def _(dve):
                ch = Chain(dve, s_dve)
                ch.link(nc.vector.memset(row[:], 0.0))
                dve.wait_ge(s_cp, 1)
                ch.link(nc.vector.tensor_tensor(ends[:, :, 0:P - 1], row[:, :, 0:P - 1], row[:, :, 1:P], ALU.not_equal))
                ch.link(nc.vector.tensor_scalar(starts[:, :, 1:P], ends[:, :, 0:P - 1], -BIG, None, ALU.mult))
                ch.link(nc.vector.memset(starts[:, :, 0:1], -BIG))
                ch.link(nc.vector.memset(ends[:, :, P - 1:P], 1.0))
                dve.wait_ge(s_iota, 1)
                ch.link(nc.vector.tensor_scalar(pick[:], gap[:].rearrange("p j c h -> p j (c h)"), 0.0, None, ALU.is_equal))


def phase_rows(nc, S, name, records, target):
    BLOCKS = [(b, min(P, NCH - b * P)) for b in range(-(-NCH // P))]
    fields = records[:].bitcast(F32)
    with Phase(nc, name) as ph:
        row = ph.sb("row", [P, len(BLOCKS), P], BF16)
        ps = ph.ps("ps", [P, 2, 4, P])
        s_tr, s_cp, s_wr = (ph.sem(n) for n in ("tr", "cp", "wr"))
        with nc.Block() as block:

            @block.tensor
            def _(pe):
                for b, n in BLOCKS:
                    mm = nc.tensor.transpose(ps[0:n, b // 4, b % 4, :], fields[:, b * P:b * P + n, 1:2].rearrange("p c o -> p (c o)"),
                                             S.ident[:])
                mm.then_inc(s_tr, 1)

            @block.scalar
            def _(act):
                act.wait_ge(s_tr, 1)
                for b, n in BLOCKS:
                    nc.scalar.copy(row[0:n, b, :], ps[0:n, b // 4, b % 4, :]).then_inc(s_cp, 1)

            @block.sync
            def _(sp):
                for b, n in BLOCKS:
                    sp.wait_ge(s_cp, b + 1)
                    sp.dma_start(target[b * P * P:(b * P + n) * P].rearrange("(n e) -> n e", e=P), row[0:n, b, :]).then_inc(s_wr, 16)
                sp.wait_ge(s_wr, len(BLOCKS) * 16)


def split(nc, ch, source, parts, rest):
    ch.link(nc.vector.tensor_copy(parts[:, :, 0, :], source))
    ch.link(nc.vector.tensor_tensor(rest, source, parts[:, :, 0, :], ALU.subtract))
    ch.link(nc.vector.tensor_copy(parts[:, :, 1, :], rest))
    ch.link(nc.vector.tensor_tensor(rest, rest, parts[:, :, 1, :], ALU.subtract))
    ch.link(nc.vector.tensor_copy(parts[:, :, 2, :], rest))


def phase_scores(nc, S, name, records, tile_of, row_of, table, field, q):
    HH = HEADS + 1
    with Phase(nc, name) as ph:
        ring = ph.sb("ring", [P, 2, GC, D])
        index = ph.sb("index", [P, 2, GC], U32)
        row = ph.sb("row", [P, 2, GC * P], BF16)
        hot = ph.sb("hot", [P, 2, GC, P])
        hot_t = ph.sb("hot_t", [P, 2, GC * P], BF16)
        q_parts = ph.sb("q_parts", [P, NT, 3, D], BF16)
        score = ph.sb("score", [P, 2, GC, HEADS])
        running = ph.sb("running", [GC * HEADS, 2, P])
        found = ph.sb("found", [P, 2, GC, HH])
        absent = ph.sb("absent", [P, GC, 1])
        top = ph.sb("top", [P, 2, GC, HEADS])
        ps_q = ph.ps("q", [P, 2, 1024])
        ps_s, ps_b, ps_x = ph.ps("s", [GC * HEADS, 512]), ph.ps("b", [P, 512]), ph.ps("x", [P, 512])
        s_gath, s_row, s_hot, s_turned, s_score, s_kept, s_sel = (
            [ph.sem(f"{n}{k}") for k in range(2)] for n in ("gath", "row", "hot", "turned", "score", "kept", "sel"))
        s_ix, s_go, s_q, s_prod, s_ts, s_scan, s_tb, s_found, s_top, s_up, s_init, s_step = (
            ph.sem(n) for n in ("ix", "go", "q", "prod", "ts", "scan", "tb", "found", "top", "up", "init", "step"))
        fields = records[:].bitcast(F32)
        flat = "p c h -> p (c h)"
        rest = S.acc[:].rearrange("p a d -> p (a d)")[:, 0:N_PAD].rearrange("p (a d) -> p a d", d=D)
        with nc.Block() as block:

            @block.gpsimd
            def _(pool):
                @each(pool, IT)
                def _(i):
                    for k in range(2):
                        if later(i):
                            pool.wait_ge(s_score[k], i)
                        nc.gpsimd.tensor_copy(index[:, k, :], records[:, bass.ds((i * 2 + k) * GC, GC), field]).then_inc(s_ix, 1)
                        pool.wait_ge(s_ix, i * 2 + k + 1)
                        pool.sem_inc(s_go, 1)
                        for c in range(GC):
                            pool.indirect_dma_start(ring[:, k, c, :], None, table,
                                                    bass.IndirectOffsetOnAxis(ap=index[:, k, c:c + 1], axis=0)).then_inc(s_gath[k], 16)

            @block.sync
            def _(sp):
                @each(sp, IT)
                def _(i):
                    for k in range(2):
                        if later(i):
                            sp.wait_ge(s_turned[k], i)
                        sp.dma_start(row[:, k, :], row_of[bass.ds((i * 2 + k) * (GC * P), GC * P)].partition_broadcast(P)).then_inc(s_row[k], 16)

            @block.vector
            def _(dve):
                def one_hot(g, k, n):
                    if later(n):
                        dve.wait_ge(s_sel[k], n)
                    nc.vector.tensor_tensor(hot[:, k], over(S.iota_row[:], GC), wide(fields[:, bass.ds(g * GC, GC), 1], P),
                                            ALU.is_equal).then_inc(s_hot[k], 1)

                def one_hot_turned(g, k, n):
                    dve.wait_ge(s_row[k], (n + 1) * 16)
                    if later(n):
                        dve.wait_ge(s_q, g - 1)
                    nc.vector.tensor_scalar(hot_t[:, k, :], row[:, k, :], S.iota_part[:, 0:1], None, ALU.is_equal).then_inc(s_turned[k], 1)

                def run_max(g, k):
                    dve.wait_ge(s_ts, g + 1)
                    nc.vector.tensor_tensor_scan(running[:, k, :], S.reset[:, bass.ds(g, 1), :].rearrange("p g e -> p (g e)"),
                                                 ps_s[:, 0:P], -BIG, ALU.add, ALU.max).then_inc(s_scan, 1)

                def find(g, k, n):
                    dve.wait_ge(s_tb, g + 1)
                    if later(n):
                        dve.wait_ge(s_sel[k], n)
                    here = S.last[:, bass.ds(g * GC, GC)]
                    nc.vector.tensor_tensor(found[:, k, :, 0:HEADS], ps_b[:, 0:GC * HEADS].rearrange("p (c h) -> p c h", h=HEADS),
                                            wide(here, HEADS), ALU.mult)
                    nc.vector.tensor_copy(found[:, k, :, HEADS:HH], here.unsqueeze(2)).then_inc(s_found, 1)

                def collect(g, k, n):
                    dve.wait_ge(s_sel[k], n + 1)
                    got = ps_x[:, 0:GC * HH].rearrange("p (c h) -> p c h", h=HH)
                    nc.vector.tensor_scalar(absent[:], got[:, :, HEADS:HH], BIG, -BIG, ALU.mult, ALU.add).then_inc(s_top, 1)
                    dve.wait_ge(s_top, g * 2 + 1)
                    nc.vector.tensor_tensor(top[:, k], got[:, :, 0:HEADS], absent[:].broadcast_to([P, GC, HEADS]), ALU.add).then_inc(s_top, 1)

                def update(g, k, tiles):
                    dve.wait_ge(s_top, g * 2 + 2)
                    for c in range(GC):
                        mx = S.mx[:, bass.ds(tiles[c], 1), :]
                        nc.vector.tensor_tensor(mx, mx, top[:, k, c:c + 1, :], ALU.max).then_inc(s_up, 1)
                        dve.wait_ge(s_up, g * GC + c + 1)

                ch = Chain(dve, s_init)
                nc.vector.memset(S.mx[:], -BIG)
                split(nc, ch, q[:], q_parts, rest)
                one_hot(0, 0, 0)
                one_hot_turned(0, 0, 0)
                one_hot_turned(1, 1, 0)

                @both_ends(dve, IT)
                def _(i, first, last):
                    if not first:
                        tiles = load_tiles(nc, mybir.EngineType.DVE, tile_of, i * 2 - 2, 2 * GC)
                    for k in range(2):
                        g = i * 2 + k
                        before = not (first and not k)
                        dve.wait_ge(s_gath[k], (i + 1) * (GC * 16))
                        dve.wait_ge(s_q, g + 1)
                        nc.vector.tensor_tensor(ring[:, k], ring[:, k], ps_q[:, k, :].rearrange("p (c d) -> p c d", d=D),
                                                ALU.mult).then_inc(s_prod, 1)
                        if before:
                            run_max(g - 1, 1 - k)
                        if later(i):
                            dve.wait_ge(s_kept[k], i)
                        dve.wait_ge(s_prod, g + 1)
                        nc.vector.tensor_reduce(score[:, k].rearrange(flat), ring[:, k].rearrange("p c (h d) -> p (c h) d", d=HS),
                                                AX_X, ALU.add).then_inc(s_score[k], 1)
                        if before:
                            find(g - 1, 1 - k, i - 1 + k)
                        if not first:
                            update(g - 2, k, tiles[k * GC:(k + 1) * GC])
                        if before:
                            collect(g - 1, 1 - k, i - 1 + k)
                        if not last:
                            one_hot_turned(g + 2, k, i + 1)
                        if not (last and k):
                            one_hot(g + 1, 1 - k, i + k)

                tiles = load_tiles(nc, mybir.EngineType.DVE, tile_of, 2 * IT - 2, 2 * GC)
                run_max(2 * IT - 1, 1)
                find(2 * IT - 1, 1, IT - 1)
                update(2 * IT - 2, 0, tiles[0:GC])
                collect(2 * IT - 1, 1, IT - 1)
                update(2 * IT - 1, 1, tiles[GC:2 * GC])

            @block.scalar
            def _(act):
                @each(act, IT)
                def _(i):
                    for k in range(2):
                        act.wait_ge(s_score[k], i + 1)
                        nc.scalar.copy(S.score_of[:, bass.ds((i * 2 + k) * GC, GC), :], score[:, k]).then_inc(s_kept[k], 1)

            @block.tensor
            def _(pe):
                def q_rows(g, k, n, tiles):
                    pe.wait_ge(s_turned[k], n + 1)
                    if later(n):
                        pe.wait_ge(s_prod, g - 1)
                    for c in range(GC):
                        for t in range(3):
                            mm = nc.tensor.matmul(ps_q[:, k, c * P:(c + 1) * P], hot_t[:, k, c * P:(c + 1) * P],
                                                  q_parts[:, bass.ds(tiles[c], 1), t, :].rearrange("p a d -> p (a d)"),
                                                  start=(t == 0), stop=(t == 2))
                    mm.then_inc(s_q, 1)

                def turn_back(g, k):
                    pe.wait_ge(s_scan, g + 1)
                    if later(g):
                        pe.wait_ge(s_found, g)
                    pe.sem_inc(s_step, 1)
                    nc.tensor.transpose(ps_b[:, 0:GC * HEADS], running[:, k, :], S.ident[0:GC * HEADS, 0:GC * HEADS]).then_inc(s_tb, 1)

                def select(g, k, n):
                    pe.wait_ge(s_found, g + 1)
                    pe.wait_ge(s_hot[k], n + 1)
                    if later(g):
                        pe.wait_ge(s_top, g * 2)
                    for c in range(GC):
                        mm = nc.tensor.matmul(ps_x[:, c * HH:(c + 1) * HH], hot[:, k, c, :], found[:, k, c, :],
                                              start=True, stop=True)
                    mm.then_inc(s_sel[k], 1)

                pe.wait_ge(s_init, 5)
                q_rows(0, 0, 0, load_tiles(nc, mybir.EngineType.PE, tile_of, 0, GC))

                @both_ends(pe, IT)
                def _(i, first, last):
                    tiles = load_tiles(nc, mybir.EngineType.PE, tile_of, i * 2 + 1, GC if last else 2 * GC)
                    for k in range(2):
                        g = i * 2 + k
                        before = not (first and not k)
                        if before:
                            turn_back(g - 1, 1 - k)
                        pe.wait_ge(s_score[k], i + 1)
                        if later(g):
                            pe.wait_ge(s_scan, g)
                        pe.sem_inc(s_step, 1)
                        nc.tensor.transpose(ps_s[:, 0:P], score[:, k].rearrange(flat), S.ident[:]).then_inc(s_ts, 1)
                        if before:
                            select(g - 1, 1 - k, i - 1 + k)
                        if not (last and k):
                            q_rows(g + 1, 1 - k, i + k, tiles[k * GC:(k + 1) * GC])

                turn_back(2 * IT - 1, 1)
                select(2 * IT - 1, 1, IT - 1)


def phase_sum(nc, S, name, H, records, tile_of, table, field, row_of=None, weight=False):
    W = D + H
    with Phase(nc, name) as ph:
        ring = ph.sb("ring", [P, 2, GC, W])
        index = ph.sb("index", [P, 2, GC], U32)
        hot = ph.sb("hot", [P, 2, GC, P])
        ps_o = ph.ps("o", [P, 2, 3, 512])
        s_gath, s_hot, s_val, s_full, s_add = ([ph.sem(f"{n}{k}") for k in range(2)] for n in ("gath", "hot", "val", "full", "add"))
        s_ix, s_init, s_go = ph.sem("ix"), ph.sem("init"), ph.sem("go")
        if H:
            row = ph.sb("row", [P, 2, GC * P], BF16)
            hot_t = ph.sb("hot_t", [P, 2, GC * P], BF16)
            mx_parts = ph.sb("mx_parts", [P, NT, 3, H], BF16)
            rest = ph.sb("rest", [P, NT, H])
            dist = ph.sb("dist", [P, 2, GC, H])
            ps_e = ph.ps("e", [P, 2, 512])
            s_row, s_turned = ([ph.sem(f"{n}{k}") for k in range(2)] for n in ("row", "turned"))
            s_me, s_dist, s_exp, s_split = (ph.sem(n) for n in ("me", "dist", "exp", "split"))
        fields = records[:].bitcast(F32)

        def sums(k, c):
            return ps_o[:, k, c // 3, (c % 3) * W:(c % 3 + 1) * W]

        with nc.Block() as block:

            @block.gpsimd
            def _(pool):
                @each(pool, IT)
                def _(i):
                    for k in range(2):
                        if later(i):
                            pool.wait_ge(s_full[k], i)
                        nc.gpsimd.tensor_copy(index[:, k, :], records[:, bass.ds((i * 2 + k) * GC, GC), field]).then_inc(s_ix, 1)
                        pool.wait_ge(s_ix, i * 2 + k + 1)
                        pool.sem_inc(s_go, 1)
                        for c in range(GC):
                            pool.indirect_dma_start(ring[:, k, c, 0:D], None, table,
                                                    bass.IndirectOffsetOnAxis(ap=index[:, k, c:c + 1], axis=0)).then_inc(s_gath[k], 16)

            if H:
                @block.sync
                def _(sp):
                    @each(sp, IT)
                    def _(i):
                        for k in range(2):
                            if later(i):
                                sp.wait_ge(s_turned[k], i)
                            sp.dma_start(row[:, k, :], row_of[bass.ds((i * 2 + k) * (GC * P), GC * P)].partition_broadcast(P)).then_inc(s_row[k], 16)

            @block.vector
            def _(dve):
                def one_hot(g, k, n):
                    if later(n):
                        dve.wait_ge(s_full[k], n)
                    nc.vector.tensor_tensor(hot[:, k], over(S.iota_row[:], GC), wide(fields[:, bass.ds(g * GC, GC), 1], P),
                                            ALU.is_equal).then_inc(s_hot[k], 1)

                def one_hot_turned(g, k, n):
                    dve.wait_ge(s_row[k], (n + 1) * 16)
                    if later(n):
                        dve.wait_ge(s_me, g - 1)
                    nc.vector.tensor_scalar(hot_t[:, k, :], row[:, k, :], S.iota_part[:, 0:1], None, ALU.is_equal).then_inc(s_turned[k], 1)

                def distance(g, k):
                    dve.wait_ge(s_me, g + 1)
                    nc.vector.tensor_tensor(dist[:, k], S.score_of[:, bass.ds(g * GC, GC), 0:H],
                                            ps_e[:, k, 0:GC * H].rearrange("p (c h) -> p c h", h=H),
                                            ALU.subtract).then_inc(s_dist, 1)

                def add_up(k, n, tiles):
                    dve.wait_ge(s_full[k], n + 1)
                    for c in range(GC):
                        a = S.acc[:, bass.ds(tiles[c], 1), 0:W]
                        nc.vector.tensor_tensor(a, a, sums(k, c).unsqueeze(1), ALU.add).then_inc(s_add[k], 1)
                        dve.wait_ge(s_add[k], n * GC + c + 1)

                nc.vector.memset(S.acc[:], 0.0).then_inc(s_init, 1)
                dve.wait_ge(s_init, 1)
                one_hot(0, 0, 0)
                if H:
                    split(nc, Chain(dve, s_split), S.mx[:, :, 0:H], mx_parts, rest[:])
                    one_hot_turned(0, 0, 0)
                    one_hot_turned(1, 1, 0)
                    distance(0, 0)

                @both_ends(dve, IT)
                def _(i, first, last):
                    if first:
                        tiles = [None] * GC + load_tiles(nc, mybir.EngineType.DVE, tile_of, 0, GC)
                    else:
                        tiles = load_tiles(nc, mybir.EngineType.DVE, tile_of, i * 2 - 1, 2 * GC)
                    for k in range(2):
                        g = i * 2 + k
                        if H:
                            dve.wait_ge(s_exp, g + 1)
                            dve.wait_ge(s_gath[k], (i + 1) * (GC * 16))
                            nc.vector.tensor_tensor(ring[:, k, :, 0:D].rearrange("p c (h d) -> p c h d", h=H),
                                                    ring[:, k, :, 0:D].rearrange("p c (h d) -> p c h d", h=H),
                                                    ring[:, k, :, D:W].unsqueeze(3).broadcast_to([P, GC, H, D // H]),
                                                    ALU.mult).then_inc(s_val[k], 1)
                            if not (last and k):
                                distance(g + 1, 1 - k)
                        elif weight:
                            dve.wait_ge(s_gath[k], (i + 1) * (GC * 16))
                            nc.vector.tensor_tensor(ring[:, k], ring[:, k], wide(fields[:, bass.ds(g * GC, GC), 2], D),
                                                    ALU.mult).then_inc(s_val[k], 1)
                        if not (last and k):
                            one_hot(g + 1, 1 - k, i + k)
                        if H and not last:
                            one_hot_turned(g + 2, k, i + 1)
                        if not (first and not k):
                            add_up(1 - k, i - 1 + k, tiles[k * GC:(k + 1) * GC])

                add_up(1, IT - 1, load_tiles(nc, mybir.EngineType.DVE, tile_of, 2 * IT - 1, GC))

            if H:
                @block.scalar
                def _(act):
                    @each(act, IT)
                    def _(i):
                        for k in range(2):
                            if later(i):
                                act.wait_ge(s_full[k], i)
                            act.wait_ge(s_dist, i * 2 + k + 1)
                            nc.scalar.activation(ring[:, k, :, D:W], dist[:, k], ACT.Exp).then_inc(s_exp, 1)

            @block.tensor
            def _(pe):
                def largest(g, k, n, tiles):
                    pe.wait_ge(s_turned[k], n + 1)
                    if later(n):
                        pe.wait_ge(s_dist, g - 1)
                    for c in range(GC):
                        for t in range(3):
                            mm = nc.tensor.matmul(ps_e[:, k, c * H:(c + 1) * H], hot_t[:, k, c * P:(c + 1) * P],
                                                  mx_parts[:, bass.ds(tiles[c], 1), t, :].rearrange("p a h -> p (a h)"),
                                                  start=(t == 0), stop=(t == 2))
                    mm.then_inc(s_me, 1)

                if H:
                    pe.wait_ge(s_split, 5)
                    largest(0, 0, 0, load_tiles(nc, mybir.EngineType.PE, tile_of, 0, GC))

                @both_ends(pe, IT)
                def _(i, first, last):
                    if H:
                        tiles = load_tiles(nc, mybir.EngineType.PE, tile_of, i * 2 + 1, GC if last else 2 * GC)
                    for k in range(2):
                        g = i * 2 + k
                        if H and not (last and k):
                            largest(g + 1, 1 - k, i + k, tiles[k * GC:(k + 1) * GC])
                        pe.wait_ge(s_hot[k], i + 1)
                        if H or weight:
                            pe.wait_ge(s_val[k], i + 1)
                        else:
                            pe.wait_ge(s_gath[k], (i + 1) * (GC * 16))
                        if later(i):
                            pe.wait_ge(s_add[k], i * GC)
                        for c in range(GC):
                            mm = nc.tensor.matmul(sums(k, c), hot[:, k, c, :], ring[:, k, c, :], start=True, stop=True)
                        mm.then_inc(s_full[k], 1)


def phase_transpose(nc, S, name, source, target):
    GROUPS = [range(a, min(a + 4, NT)) for a in range(0, NT, 4)]
    with Phase(nc, name) as ph:
        ps = ph.ps("ps", [P, 2, 512])
        s_tr, s_cp = ph.sem("tr"), ph.sem("cp")
        with nc.Block() as block:

            @block.tensor
            def _(pe):
                for g, tiles in enumerate(GROUPS):
                    if g >= 2:
                        pe.wait_ge(s_cp, g - 1)
                    for c, a in enumerate(tiles):
                        mm = nc.tensor.transpose(ps[:, g % 2, c * P:(c + 1) * P], source[:, a, :], S.ident[:])
                    mm.then_inc(s_tr, 1)

            @block.scalar
            def _(act):
                for g, tiles in enumerate(GROUPS):
                    act.wait_ge(s_tr, g + 1)
                    n = len(tiles) * P
                    nc.scalar.copy(target[:, g * 512:g * 512 + n], ps[:, g % 2, 0:n]).then_inc(s_cp, 1)


def phase_expand(nc, S, name, source_t, matrix, table):
    C = matrix.shape[1]
    U, TI, RING = C // 512, 5, 5
    rows = table.rearrange("(a p t) d -> a p (t d)", p=P, a=NT)
    with Phase(nc, name) as ph:
        left = ph.sb("left", [P, TI, P])
        out = ph.sb("out", [P, RING, 512])
        ps = ph.ps("ps", [P, RING, 512])
        s_left = ph.sem("left")
        s_mm, s_ev, s_wr = ([ph.sem(f"{n}{r}") for r in range(RING)] for n in ("mm", "ev", "wr"))

        def evacuate(eng, copy, i, u):
            r, n = u % RING, i * U + u // RING
            eng.wait_ge(s_mm[r], n + 1)
            if later(n * 16):
                eng.wait_ge(s_wr[r], n * 16)
            copy(out[:, r, :], ps[:, r, :]).then_inc(s_ev[r], 1)

        with nc.Block() as block:

            @block.vector
            def _(dve):
                @each(dve, NT // TI)
                def _(i):
                    if later(i * U):
                        dve.wait_ge(s_mm[RING - 1], i * U)
                    nc.vector.tensor_copy(left[:].rearrange("p a n -> p (a n)"),
                                          source_t[:, bass.ds(i * (TI * P), TI * P)]).then_inc(s_left, 1)
                    for u in range(0, TI * U, 2):
                        evacuate(dve, nc.vector.tensor_copy, i, u)

            @block.scalar
            def _(act):
                @each(act, NT // TI)
                def _(i):
                    for u in range(1, TI * U, 2):
                        evacuate(act, nc.scalar.copy, i, u)

            @block.tensor
            def _(pe):
                @each(pe, NT // TI)
                def _(i):
                    pe.wait_ge(s_left, i + 1)
                    for u in range(TI * U):
                        r, n = u % RING, i * U + u // RING
                        if later(n):
                            pe.wait_ge(s_ev[r], n)
                        nc.tensor.matmul(ps[:, r, :], left[:, u // U, :], matrix[:, (u % U) * 512:(u % U + 1) * 512],
                                         start=True, stop=True).then_inc(s_mm[r], 1)

            @block.sync
            def _(sp):
                @each(sp, NT // TI)
                def _(i):
                    for u in range(TI * U):
                        r, n = u % RING, i * U + u // RING
                        sp.wait_ge(s_ev[r], n + 1)
                        sp.dma_start(rows[bass.ds(i * TI + u // U, 1), :, (u % U) * 512:(u % U + 1) * 512].rearrange("a p c -> (a p) c"),
                                     out[:, r, :]).then_inc(s_wr[r], 16)
                for r in range(RING):
                    sp.wait_ge(s_wr[r], (NT // TI) * U * 16)


def phase_typed(nc, S, name, source_t, weights, node_type, outs):
    n_out, HALF = len(outs), R16 // 2
    with Phase(nc, name) as ph:
        w = ph.sb("w", [P, n_out, R16, P])
        types = ph.sb("types", [P, N_PAD], I32)
        only = ph.sb("only", [P, R16, P])
        ps = [ph.ps(f"ps{o}", [P, 512]) for o in range(n_out)]
        s_in, s_ev = ph.sem("in"), ph.sem("ev")
        s_only, s_mm = ([ph.sem(f"{n}{k}") for k in range(2)] for n in ("only", "mm"))
        with nc.Block() as block:

            @block.sync
            def _(sp):
                sp.dma_start(types[:], node_type.partition_broadcast(P)).then_inc(s_in, 16)
                for o, weight in enumerate(weights):
                    sp.dma_start(w[:, o], weight.rearrange("t d o -> d t o")).then_inc(s_in, 16)

            @block.vector
            def _(dve):
                dve.wait_ge(s_in, 16 * (1 + n_out))
                @each(dve, NT)
                def _(a):
                    cols = bass.ds(a * P, P)
                    for k in range(2):
                        if later(a):
                            dve.wait_ge(s_mm[k], a)
                        for t in range(k * HALF, (k + 1) * HALF):
                            ins = nc.vector.scalar_tensor_tensor(out=only[:, t, :], in0=types[:, cols], scalar=float(t),
                                                                 in1=source_t[:, cols], op0=ALU.is_equal, op1=ALU.mult)
                        ins.then_inc(s_only[k], 1)

            @block.tensor
            def _(pe):
                pe.wait_ge(s_in, 16 * (1 + n_out))
                @each(pe, NT)
                def _(a):
                    if later(a * n_out):
                        pe.wait_ge(s_ev, a * n_out)
                    for k in range(2):
                        pe.wait_ge(s_only[k], a + 1)
                        for t in range(k * HALF, (k + 1) * HALF):
                            for o, (_, across, _) in enumerate(outs):
                                left, right = (w[:, o, t, :], only[:, t, :]) if across else (only[:, t, :], w[:, o, t, :])
                                mm = nc.tensor.matmul(ps[o][:, 0:P], left, right, start=(t == 0), stop=(t == R16 - 1))
                        mm.then_inc(s_mm[k], 1)

            @block.scalar
            def _(act):
                @each(act, NT)
                def _(a):
                    act.wait_ge(s_mm[1], a + 1)
                    for o, (target, _, function) in enumerate(outs):
                        nc.scalar.activation(target[:, bass.ds(a * P, P)], ps[o][:, 0:P], function).then_inc(s_ev, 1)


def phase_heads(nc, S, name, matrix, weight, pri=None):
    with Phase(nc, name) as ph:
        scale = ph.sb("scale", [P, R32])
        s_zero, s_in, s_dve = ph.sem("zero"), ph.sem("in"), ph.sem("dve")
        n_in = 16 * HEADS * (1 if pri is None else 2)
        m = matrix[:].rearrange("p (t o) -> p t o", o=P)
        with nc.Block() as block:

            @block.sync
            def _(sp):
                sp.wait_ge(s_zero, 1)
                for h in range(HEADS):
                    at = slice(h * HS, (h + 1) * HS)
                    sp.dma_start(m[at, :, at], weight[h].rearrange("t d o -> d t o")).then_inc(s_in, 16)
                    if pri is not None:
                        sp.dma_start(scale[at, :], pri[h].partition_broadcast(HS)).then_inc(s_in, 16)
                sp.wait_ge(s_in, n_in)

            @block.vector
            def _(dve):
                nc.vector.memset(matrix[:], 0.0).then_inc(s_zero, 1)
                if pri is not None:
                    ch = Chain(dve, s_dve)
                    dve.wait_ge(s_in, n_in)
                    ch.link(nc.vector.tensor_scalar(scale[:], scale[:], float(HS) ** -0.5, None, ALU.mult))
                    ch.link(nc.vector.tensor_tensor(m, m, wide(scale[:], P), ALU.mult))


def phase_scaled_table(nc, S, name, source, target, table):
    with Phase(nc, name) as ph:
        s_dve, s_wr = ph.sem("dve"), ph.sem("wr")
        with nc.Block() as block:

            @block.vector
            def _(dve):
                nc.vector.tensor_tensor(target[:], source[:], wide(S.dinv[:], D), ALU.mult).then_inc(s_dve, 1)

            @block.sync
            def _(sp):
                sp.wait_ge(s_dve, 1)
                sp.dma_start(table.rearrange("(a p) d -> p a d", p=P), target[:]).then_inc(s_wr, 16)
                sp.wait_ge(s_wr, 16)


def phase_gcn_dense(nc, S, source_t, W1, b1, W2, target):
    HB = HID // P
    with Phase(nc, "gcn") as ph:
        w1 = ph.sb("w1", [P, HID])
        w2 = ph.sb("w2", [P, HB, D])
        bias = ph.sb("bias", [P, HB])
        hidden = ph.sb("hidden", [P, HB, P])
        ps_h = ph.ps("h", [P, HB, 512])
        ps_o = ph.ps("o", [P, 512])
        s_in, s_h, s_act, s_o, s_ev = (ph.sem(n) for n in ("in", "h", "act", "o", "ev"))
        with nc.Block() as block:

            @block.sync
            def _(sp):
                sp.dma_start(w1[:], W1).then_inc(s_in, 16)
                sp.dma_start(w2[:], W2.rearrange("(h p) o -> p h o", p=P)).then_inc(s_in, 16)
                for h in range(HB):
                    sp.dma_start(bias[:, h:h + 1], b1[h * P:(h + 1) * P].unsqueeze(1)).then_inc(s_in, 16)

            @block.tensor
            def _(pe):
                pe.wait_ge(s_in, 64)
                @each(pe, NT)
                def _(a):
                    for h in range(HB):
                        if later(a * HB):
                            pe.wait_ge(s_act, a * HB)
                        nc.tensor.matmul(ps_h[:, h, 0:P], w1[:, h * P:(h + 1) * P], source_t[:, bass.ds(a * P, P)],
                                         start=True, stop=True).then_inc(s_h, 1)
                    if later(a):
                        pe.wait_ge(s_ev, a)
                    pe.wait_ge(s_act, (a + 1) * HB)
                    for h in range(HB):
                        mm = nc.tensor.matmul(ps_o[:, 0:D], hidden[:, h, :], w2[:, h, :], start=(h == 0), stop=(h == HB - 1))
                    mm.then_inc(s_o, 1)

            @block.scalar
            def _(act):
                act.wait_ge(s_in, 64)
                @each(act, NT)
                def _(a):
                    if later(a):
                        act.wait_ge(s_o, a)
                    for h in range(HB):
                        act.wait_ge(s_h, a * HB + h + 1)
                        nc.scalar.activation(hidden[:, h, :], ps_h[:, h, 0:P], ACT.Relu, bias=bias[:, h:h + 1]).then_inc(s_act, 1)

            @block.vector
            def _(dve):
                @each(dve, NT)
                def _(a):
                    dve.wait_ge(s_o, a + 1)
                    nc.vector.tensor_copy(target[:, bass.ds(a, 1), :], ps_o[:, 0:D].unsqueeze(1)).then_inc(s_ev, 1)


def normalize(ph, nc, S, dve, ch, y, out):
    mean = ph.sb("mean", [P, NT])
    square = ph.sb("square", [P, NT, D])
    ch.link(nc.vector.tensor_reduce(mean[:], y, AX_X, ALU.add))
    ch.link(nc.vector.tensor_scalar(mean[:], mean[:], 1.0 / D, None, ALU.mult))
    ch.link(nc.vector.tensor_tensor(out, y, wide(mean[:], D), ALU.subtract))
    ch.link(nc.vector.tensor_tensor(square[:], out, out, ALU.mult))
    ch.link(nc.vector.tensor_reduce(S.var[:], square[:], AX_X, ALU.add))
    ready = ch.n
    dve.wait_ge(ph.s_root, 1)
    ch.link(nc.vector.reciprocal(S.var[:], S.var[:]))
    ch.link(nc.vector.tensor_tensor(out, out, wide(S.var[:], D), ALU.mult))
    return ready


def phase_norm(nc, S, name, prepare, out, loads=(), finish=None, bias=None, alpha=None):
    with Phase(nc, name) as ph:
        y = ph.sb("y", [P, NT, D])
        s_dve, s_in = ph.sem("dve"), ph.sem("in")
        ph.s_root, ph.s_alpha = ph.sem("root"), ph.sem("alpha")
        count = {}
        with nc.Block() as block:

            if loads:
                @block.sync
                def _(sp):
                    for target, source in loads:
                        sp.dma_start(target, source).then_inc(s_in, 16)

            @block.vector
            def _(dve):
                ch = Chain(dve, s_dve)
                if loads:
                    dve.wait_ge(s_in, 16 * len(loads))
                count["alpha"] = prepare(dve, ch, y, ph)
                count["var"] = normalize(ph, nc, S, dve, ch, y[:], out[:])
                if finish:
                    finish(ch)

            @block.scalar
            def _(act):
                if alpha is not None:
                    act.wait_ge(s_dve, count["alpha"])
                    nc.scalar.activation(alpha[:], alpha[:], ACT.Sigmoid).then_inc(ph.s_alpha, 1)
                act.wait_ge(s_dve, count["var"])
                nc.scalar.activation(S.var[:], S.var[:], ACT.Sqrt, bias=S.eps[:, 0:1], scale=1.0 / D).then_inc(ph.s_root, 1)


def phase_output(nc, S, source_t, weight, bias, out):
    GROUPS = [range(a, min(a + 4, NT)) for a in range(0, NT, 4)]
    with Phase(nc, "head") as ph:
        w = ph.sb("w", [P, D])
        b = ph.sb("b", [P, D])
        ps = ph.ps("ps", [P, 2, 512])
        s_in, s_mm, s_ev = ph.sem("in"), ph.sem("mm"), ph.sem("ev")
        with nc.Block() as block:

            @block.sync
            def _(sp):
                sp.dma_start(w[:], weight).then_inc(s_in, 16)
                sp.dma_start(b[:], bias.partition_broadcast(P)).then_inc(s_in, 16)

            @block.tensor
            def _(pe):
                pe.wait_ge(s_in, 32)
                for g, tiles in enumerate(GROUPS):
                    if g >= 2:
                        pe.wait_ge(s_ev, g - 1)
                    for c, a in enumerate(tiles):
                        mm = nc.tensor.matmul(ps[:, g % 2, c * P:(c + 1) * P], source_t[:, a * P:(a + 1) * P], w[:], start=True, stop=True)
                    mm.then_inc(s_mm, 1)

            @block.vector
            def _(dve):
                dve.wait_ge(s_in, 32)
                for g, tiles in enumerate(GROUPS):
                    dve.wait_ge(s_mm, g + 1)
                    n = len(tiles)
                    nc.vector.tensor_tensor(S.h[:, g * 4:g * 4 + n, :], ps[:, g % 2, 0:n * P].rearrange("p (a d) -> p a d", d=D),
                                            over(b[:], n), ALU.add).then_inc(s_ev, 1)
    def residual(dve, ch, y, ph):
        ch.link(nc.vector.tensor_tensor(y[:], S.x[:], S.h[:], ALU.add))

    phase_norm(nc, S, "last", residual, S.x)
    with Phase(nc, "store") as ph:
        s_wr = ph.sem("wr")
        with nc.Block() as block:

            @block.sync
            def _(sp):
                full = N_NODES // P
                sp.dma_start(out[0:full * P, :].rearrange("(a p) d -> p a d", p=P), S.x[:, 0:full, :]).then_inc(s_wr, 16)
                sp.dma_start(out[full * P:N_NODES, :], S.x[0:N_NODES - full * P, full, :]).then_inc(s_wr, 16)
                sp.wait_ge(s_wr, 32)


class Arrays:
    pass


def gnn_program(nc, A, out):
    S = Arrays()
    main = ExitStack()

    def sb(scope, name, shape, dt=F32):
        return scope.enter_context(nc.sbuf_tensor(name, shape, dt))

    def dram(name, shape, dt=F32):
        return nc.dram_tensor(name, shape, dt, kind="Internal").ap()

    rec_d_dram, rec_s_dram = dram("rec_d_dram", (NSLOT, RD), I32), dram("rec_s_dram", (NSLOT, RS), I32)
    row_d, row_s = dram("row_d", (NSLOT,), BF16), dram("row_s", (NSLOT,), BF16)
    rows = dram("rows", (N_PAD, D))
    rows8 = dram("rows8", (N_PAD * R8, D))
    k_rows, v_rows = dram("k_rows", (N_PAD * R32, D)), dram("v_rows", (N_PAD * R32, D))

    with main:
        S.iota_row, S.iota_part = sb(main, "iota_row", [P, P]), sb(main, "iota_part", [P, 1])
        S.ident, S.before, S.ones = sb(main, "ident", [P, P]), sb(main, "before", [P, P]), sb(main, "ones", [P, P])
        S.ident4_bf, S.eps = sb(main, "ident4_bf", [P, 4, P], BF16), sb(main, "eps", [P, 1])
        S.sel1 = sb(main, "sel1", [3, P], BF16)
        S.x, S.h = sb(main, "x", [P, NT, D]), sb(main, "h", [P, NT, D])
        S.acc = sb(main, "acc", [P, NT, D + HEADS])
        S.dinv, S.var = sb(main, "dinv", [P, NT]), sb(main, "var", [P, NT])
        S.mx = sb(main, "mx", [P, NT, HEADS])
        rec_d, tile_d = sb(main, "rec_d", [P, NCH, RD], I32), sb(main, "tile_d", [1, NCH], I32)

        with ExitStack() as first:
            rec_s, tile_s = sb(first, "rec_s", [P, NCH, RS], I32), sb(first, "tile_s", [1, NCH], I32)
            S.score_of = sb(first, "score_of0", [P, NCH, 1])
            S.chunk_no = sb(first, "chunk_no", [NT, NCH])
            phase_constants(nc, S, A["x"])
            with ExitStack() as edges:
                S.raw, S.weight = sb(edges, "raw", [P, 7, EC], I32), sb(edges, "weight", [P, EC])
                S.src_a, S.src_b, S.dst_a, S.dst_b, S.rel_high, S.score, S.tmp_f = (
                    sb(edges, name, [P, EC]) for name in ("src_a", "src_b", "dst_a", "dst_b", "rel_high", "score", "tmp_f"))
                S.tmp_i, S.row32, S.row8, slot_s, slot_d = (
                    sb(edges, name, [P, EC], I32) for name in ("tmp_i", "row32", "row8", "slot_s", "slot_d"))
                phase_edges(nc, S, A, ((rec_s, rec_s_dram), (rec_d, rec_d_dram)))
                pack_s, pack_d = sb(edges, "pack_s", [P, EC, RS], I32), sb(edges, "pack_d", [P, EC, RD], I32)
                phase_rank(nc, S, "rank_s", rank_program(
                    nc, S, S.src_a, slot_s, tile_s, pack_s, ((I32, S.raw[:, 3, :]), (F32, S.src_b[:]), (F32, S.score[:]))))
                phase_scatter(nc, S, "scat_s", slot_s, pack_s, RS, rec_s_dram, rec_s, rank_program(
                    nc, S, S.dst_a, slot_d, tile_d, pack_d,
                    ((I32, S.raw[:, 2, :]), (F32, S.dst_b[:]), (F32, S.weight[:]), (I32, S.row8[:]), (I32, S.row32[:]))))
                phase_scatter(nc, S, "scat_d", slot_d, pack_d, RD, rec_d_dram, rec_d, max_program(nc, S, rec_s, tile_s))

            phase_rows(nc, S, "rows_s", rec_s, row_s)
            phase_sum(nc, S, "sum0", 1, rec_s, tile_s, A["x"], 0, row_s)

        def after_attention(dve, ch, y, ph):
            total = ph.sb("total", [P, NT])
            ch.link(nc.vector.tensor_scalar(total[:], S.acc[:, :, D:D + 1].rearrange("p a o -> p (a o)"), 1e-30, None, ALU.max))
            ch.link(nc.vector.reciprocal(total[:], total[:]))
            ch.link(nc.vector.tensor_tensor(y[:], S.acc[:, :, 0:D], wide(total[:], D), ALU.mult))
            ch.link(nc.vector.scalar_tensor_tensor(out=y[:], in0=y[:], scalar=0.0, in1=S.x[:], op0=ALU.max, op1=ALU.add))
            ch.link(nc.vector.reciprocal(S.dinv[:], S.dinv[:]))

        phase_norm(nc, S, "norm0", after_attention, S.x)

        S.last, S.reset = sb(main, "last", [P, NCH]), sb(main, "reset", [GC * HEADS, NCH // GC, P], BF16)
        phase_order(nc, S, rec_d, dram("key_dram", (NSLOT,)))
        phase_segments(nc, S, rec_d)
        phase_rows(nc, S, "rows_d", rec_d, row_d)

        with ExitStack() as gcn:
            t = sb(gcn, "t", [P, NT, D])
            xt = sb(gcn, "xt1", [P, N_PAD])
            bias = sb(gcn, "b2", [P, D])
            phase_scaled_table(nc, S, "table1", S.x, t, rows)
            phase_sum(nc, S, "sum1", 0, rec_d, tile_d, rows, 0)
            with Phase(nc, "self1") as ph:
                s_dve = ph.sem("dve")
                with nc.Block() as block:

                    @block.vector
                    def _(dve):
                        ch = Chain(dve, s_dve)
                        ch.link(nc.vector.tensor_tensor(t[:], t[:], S.acc[:, :, 0:D], ALU.add))
                        ch.link(nc.vector.tensor_tensor(t[:], t[:], wide(S.dinv[:], D), ALU.mult))

            phase_transpose(nc, S, "tr1", t, xt)
            phase_gcn_dense(nc, S, xt, A["W1"], A["b1"], A["W2"], S.h)
            phase_scaled_table(nc, S, "table2", S.h, t, rows)
            phase_sum(nc, S, "sum2", 0, rec_d, tile_d, rows, 0)

            def after_gcn(dve, ch, y, ph):
                ch.link(nc.vector.tensor_tensor(t[:], t[:], S.acc[:, :, 0:D], ALU.add))
                ch.link(nc.vector.tensor_tensor(t[:], t[:], wide(S.dinv[:], D), ALU.mult))
                ch.link(nc.vector.tensor_tensor(t[:], t[:], over(bias[:], NT), ALU.add))
                ch.link(nc.vector.scalar_tensor_tensor(out=y[:], in0=t[:], scalar=0.0, in1=S.x[:], op0=ALU.max, op1=ALU.add))

            phase_norm(nc, S, "norm1", after_gcn, S.x, loads=((bias[:], A["b2"].partition_broadcast(P)),))

        with ExitStack() as rgcn:
            xt = sb(rgcn, "xt2", [P, N_PAD])
            matrix = sb(rgcn, "matrix2", [P, R8 * D])
            with Phase(nc, "load2") as ph:
                s_in = ph.sem("in")
                with nc.Block() as block:

                    @block.sync
                    def _(sp):
                        sp.dma_start(matrix[:].rearrange("p (t o) -> p t o", t=R8), A["rel_emb"].rearrange("t d o -> d t o")).then_inc(s_in, 16)
                        sp.wait_ge(s_in, 16)

            phase_transpose(nc, S, "tr2", S.x, xt)
            phase_expand(nc, S, "expand2", xt, matrix, rows8)
        phase_sum(nc, S, "sum3", 0, rec_d, tile_d, rows8, 3, weight=True)

        def after_rgcn(dve, ch, y, ph):
            ch.link(nc.vector.tensor_tensor(y[:], S.x[:], S.acc[:, :, 0:D], ALU.add))

        phase_norm(nc, S, "norm2", after_rgcn, S.x)

        for layer in range(LAYERS):
            old = S.x if layer == 0 else S.h
            with ExitStack() as hgt:
                q = sb(hgt, f"q{layer}", [P, NT, D])
                with ExitStack() as pre:
                    kt, vt = S.acc[:].rearrange("p a d -> p (a d)")[:, 0:N_PAD], sb(pre, f"vt{layer}", [P, N_PAD])
                    with ExitStack() as tr:
                        xt = sb(tr, f"xt3{layer}", [P, N_PAD])
                        phase_transpose(nc, S, f"tr3{layer}", old, xt)
                        phase_typed(nc, S, f"kqv{layer}", xt, [A["Wk"][layer], A["Wq"][layer], A["Wv"][layer]], A["node_type"],
                                    [(kt, True, ACT.Copy), (q[:].rearrange("p a d -> p (a d)"), False, ACT.Copy), (vt, True, ACT.Copy)])
                    matrix = sb(pre, f"matrix3{layer}", [P, R32 * D])
                    phase_heads(nc, S, f"att{layer}", matrix, A["Watt"][layer], A["pri"][layer])
                    phase_expand(nc, S, f"expk{layer}", kt, matrix, k_rows)
                    phase_heads(nc, S, f"msg{layer}", matrix, A["Wmsg"][layer])
                    phase_expand(nc, S, f"expv{layer}", vt, matrix, v_rows)
                S.score_of = sb(hgt, f"score_of{layer + 1}", [P, NCH, HEADS])
                phase_scores(nc, S, f"max{layer + 1}", rec_d, tile_d, row_d, k_rows, 4, q)
                phase_sum(nc, S, f"sum{layer + 4}", HEADS, rec_d, tile_d, v_rows, 4, row_d)
            with ExitStack() as post:
                hag = sb(post, f"hag{layer}", [P, NT, D])
                xt = sb(post, f"xt4{layer}", [P, N_PAD])
                with Phase(nc, f"hag_{layer}") as ph:
                    s_dve = ph.sem("dve")
                    total = ph.sb("total", [P, NT, HEADS])
                    with nc.Block() as block:

                        @block.vector
                        def _(dve):
                            ch = Chain(dve, s_dve)
                            ch.link(nc.vector.tensor_scalar(total[:], S.acc[:, :, D:D + HEADS], 1e-30, None, ALU.max))
                            ch.link(nc.vector.reciprocal(total[:], total[:]))
                            for h in range(HEADS):
                                at = slice(h * HS, (h + 1) * HS)
                                ins = nc.vector.tensor_tensor(hag[:, :, at], S.acc[:, :, at],
                                                              total[:, :, h:h + 1].broadcast_to([P, NT, HS]), ALU.mult)
                            ch.link(ins)

                phase_transpose(nc, S, f"tr4{layer}", hag, xt)
                phase_typed(nc, S, f"wa{layer}", xt, [A["Wa"][layer]], A["node_type"],
                            [(hag[:].rearrange("p a d -> p (a d)"), False, ACT.Silu)])
                alpha = sb(post, f"alpha{layer}", [P, NT])
                type_i = sb(post, f"type_i{layer}", [P, NT], I32)
                skip = sb(post, f"skip{layer}", [P, R16])
                gain, shift = sb(post, f"gain{layer}", [P, D]), sb(post, f"shift{layer}", [P, D])
                hot = sb(post, f"hot{layer}", [P, NT, R16])

                def mix(dve, ch, y, ph):
                    ch.link(nc.vector.tensor_copy(alpha[:], type_i[:]))
                    ch.link(nc.vector.tensor_tensor(hot[:], over(S.iota_row[:, 0:R16], NT), wide(alpha[:], R16), ALU.is_equal))
                    ch.link(nc.vector.tensor_tensor(hot[:], hot[:], over(skip[:], NT), ALU.mult))
                    ch.link(nc.vector.tensor_reduce(alpha[:], hot[:], AX_X, ALU.add))
                    ready = ch.n
                    dve.wait_ge(ph.s_alpha, 1)
                    ch.link(nc.vector.tensor_tensor(y[:], hag[:], old[:], ALU.subtract))
                    ch.link(nc.vector.tensor_tensor(y[:], y[:], wide(alpha[:], D), ALU.mult))
                    ch.link(nc.vector.tensor_tensor(y[:], y[:], old[:], ALU.add))
                    return ready

                def affine(ch):
                    ch.link(nc.vector.tensor_tensor(S.h[:], S.h[:], over(gain[:], NT), ALU.mult))
                    ch.link(nc.vector.tensor_tensor(S.h[:], S.h[:], over(shift[:], NT), ALU.add))

                phase_norm(nc, S, f"norm3{layer}", mix, S.h, finish=affine, alpha=alpha,
                           loads=((type_i[:], A["node_col"]), (skip[:], A["skip"][layer].partition_broadcast(P)),
                                  (gain[:], A["ln_g"][layer].partition_broadcast(P)), (shift[:], A["ln_b"][layer].partition_broadcast(P))))
        with ExitStack() as end:
            xt = sb(end, "xt5", [P, N_PAD])
            phase_transpose(nc, S, "tr5", S.h, xt)
            phase_output(nc, S, xt, A["ff_w"], A["ff_b"], out)


def kernel(**inputs):
    import concourse.bacc as _bacc
    from concourse.bass_utils import run_bass_kernel_spmd as _run

    def column(a, pad):
        flat = np.full(EC * P, pad, a.dtype)
        flat[:N_EDGES] = a
        return np.ascontiguousarray(flat.reshape(EC, P).T)

    def padded(a, n):
        out = np.zeros((n,) + a.shape[1:], a.dtype)
        out[:a.shape[0]] = a
        return out

    g = {k: np.asarray(v) for k, v in inputs.items()}
    types = padded(g["node_type_16"], N_PAD)
    arrays = {
        "x": padded(g["x"], N_PAD), "node_type": types, "node_col": np.ascontiguousarray(types.reshape(NT, P).T),
        "src_key": column(g["src"], N_PAD), "dst_key": column(g["dst"], N_PAD),
        "src_val": column(g["src"], 0), "dst_val": column(g["dst"], 0),
        "rel": column(g["edge_type_1000"], 0), "rel_flat": padded(g["edge_type_1000"], EC * P),
        "type32": column(g["edge_type_32"], 0), "type8": column(g["edge_type_8"], 0), "weight": column(g["edge_weight"], 0),
        "dual_layer": g["L0_gnn_dual_layer"], "conv_w": g["L0_gnn_conv_w"], "conv_b": g["L0_gnn_conv_b"],
        "W1": g["L1_gnn_W1"], "b1": g["L1_gnn_b1"], "W2": g["L1_gnn_W2"], "b2": g["L1_gnn_b2"],
        "rel_emb": g["L2_gnn_rel_emb"],
    }
    for name in ("Wk", "Wq", "Wv", "Wa", "Watt", "Wmsg", "pri", "skip", "ln_g", "ln_b", "ff_w", "ff_b"):
        arrays[name] = g["L3_gnn_" + name]

    nc = _bacc.Bacc("TRN2", target_bir_lowering=False, num_devices=1)
    arrays = {f"in_{n}": np.ascontiguousarray(a) for n, a in arrays.items()}
    A = {n[3:]: nc.dram_tensor(n, a.shape, mybir.dt.from_np(a.dtype), kind="ExternalInput").ap() for n, a in arrays.items()}
    out = nc.dram_tensor("out_0", (N_NODES, D), F32, kind="ExternalOutput").ap()
    gnn_program(nc, A, out)
    r = _run(nc, [arrays], core_ids=[0])
    return r.results[0]["out_0"]
```
